# Optimizing a Trainium2 kernel written in Bass

```python
import numpy as np
import jax
import jax.numpy as jnp

def _softmax(x, axis=-1):
    return jax.nn.softmax(x, axis=axis)

def _gelu(x):
    return jax.nn.gelu(x, approximate=True)

def _silu(x):
    return jax.nn.silu(x)

def _sigmoid(x):
    return jax.nn.sigmoid(x)

def _layernorm(x, axis=-1, eps=1e-05):
    m = jnp.mean(x, axis=axis, keepdims=True)
    v = jnp.var(x, axis=axis, keepdims=True)
    return (x - m) / jnp.sqrt(v + eps)

def _scatter_add(tgt, idx, src, axis=0):
    return tgt.at[idx].add(src)

def _segment_sum(src, seg, n):
    return jax.ops.segment_sum(src, seg, n)
kernel_name = 'mk_gnn_resnorm_d2_gnn_r32_963aa8'

def setup_inputs(seed: int=0):
    np.random.seed(seed)
    _w = jnp.asarray

    def _rec_inputs():
        import jax
        import jax.numpy as jnp
        _gk = jax.random.key(seed)
        x = -0.000202 + 1 * jax.random.normal(jax.random.fold_in(_gk, 1), (50000, 128), jnp.float32)
        src = jax.random.randint(jax.random.fold_in(_gk, 2), (25000,), 0, 50000, jnp.int32)
        dst = jax.random.randint(jax.random.fold_in(_gk, 3), (25000,), 0, 50000, jnp.int32)
        _o = jnp.argsort(dst, stable=True)
        src = src[_o]
        dst = dst[_o]
        edge_type_30 = jax.random.randint(jax.random.fold_in(_gk, 12), (25000,), 0, 30, jnp.int32)
        edge_weight = jax.random.uniform(jax.random.fold_in(_gk, 13), (25000,), jnp.float32, 0.0, 0.999998)
        return (x, src, dst, edge_type_30, edge_weight)
    x, src, dst, edge_type_30, edge_weight = _rec_inputs()

    def _L0_gnn_setup():
        import jax, jax.numpy as jnp
        import numpy as np
        N, E, D, L = (50000, 25000, 128, 3)
        key = jax.random.key(seed)
        ks = jax.random.split(key, 6)
        x = jax.random.normal(ks[0], (N, D), dtype=jnp.float32)
        edge_index = jax.random.randint(ks[1], (2, E), 0, N, dtype=jnp.int64)
        edge_weight = jax.random.uniform(ks[2], (E,), dtype=jnp.float32)
        s = 1.0 / np.sqrt(D)
        W_rel = jax.random.uniform(ks[3], (L, D, D), dtype=jnp.float32, minval=-s, maxval=s)
        b_rel = jax.random.uniform(ks[4], (L, D), dtype=jnp.float32, minval=-s, maxval=s)
        W_root = jax.random.uniform(ks[5], (L, D, D), dtype=jnp.float32, minval=-s, maxval=s)
        return {'x': x, 'edge_index': edge_index, 'edge_weight': edge_weight, 'W_rel': W_rel, 'b_rel': b_rel, 'W_root': W_root}
    _L0_gnn_all = _L0_gnn_setup()
    _L0_gnn_in = {k: v for k, v in _L0_gnn_all.items() if k in ('W_rel', 'b_rel', 'W_root')}
    del _L0_gnn_all

    def _L1_gnn_setup():
        import jax, jax.numpy as jnp
        import numpy as np
        N_NODES = 50000
        N_EDGES = 18750
        D_IN = 128
        D_OUT = 128
        NUM_REL = 10
        key = jax.random.key(seed)
        k_x, k_ei, k_et, k_w, k_b = jax.random.split(key, 5)
        x = jax.random.normal(k_x, (N_NODES, D_IN), dtype=jnp.float32)
        edge_index = jax.random.randint(k_ei, (2, N_EDGES), 0, N_NODES, dtype=jnp.int64)
        edge_types = jax.random.randint(k_et, (N_EDGES,), 0, 3 * NUM_REL, dtype=jnp.int64)
        bound = 1.0 / np.sqrt(D_IN)
        W = jax.random.uniform(k_w, (3, D_IN, D_OUT), minval=-bound, maxval=bound, dtype=jnp.float32)
        b = jax.random.uniform(k_b, (3, D_OUT), minval=-bound, maxval=bound, dtype=jnp.float32)
        return {'x': x, 'edge_index': edge_index, 'edge_types': edge_types, 'W': W, 'b': b}
    _L1_gnn_all = _L1_gnn_setup()
    _L1_gnn_in = {k: v for k, v in _L1_gnn_all.items() if k in ('W', 'b')}
    del _L1_gnn_all
    return {'x': x, 'src': src, 'dst': dst, 'edge_type_30': edge_type_30, 'edge_weight': edge_weight, 'L0_gnn_W_rel': _L0_gnn_in['W_rel'], 'L0_gnn_b_rel': _L0_gnn_in['b_rel'], 'L0_gnn_W_root': _L0_gnn_in['W_root'], 'L1_gnn_W': _L1_gnn_in['W'], 'L1_gnn_b': _L1_gnn_in['b']}

def reference(x, src, dst, edge_type_30, edge_weight, L0_gnn_W_rel, L0_gnn_b_rel, L0_gnn_W_root, L1_gnn_W, L1_gnn_b):
    import jax
    import jax.numpy as jnp

    def _L0_gnn_ref(x, edge_index, edge_weight, W_rel, b_rel, W_root):
        import jax, jax.numpy as jnp
        import numpy as np
        N, E, D, L = (50000, 25000, 128, 3)
        src, dst = (edge_index[0], edge_index[1])

        def conv(h, i):
            msg = h[src] * edge_weight[:, None]
            agg = jax.ops.segment_sum(msg, dst, num_segments=N)
            return agg @ W_rel[i] + b_rel[i] + h @ W_root[i]
        h = x
        for i in range(L - 1):
            h = jax.nn.relu(conv(h, i))
        return conv(h, L - 1)

    def _L1_gnn_ref(x, edge_index, edge_types, W, b):
        import jax, jax.numpy as jnp
        import numpy as np
        N_NODES = 50000
        N_EDGES = 18750
        D_IN = 128
        D_OUT = 128
        NUM_REL = 10
        src, dst = (edge_index[0], edge_index[1])
        src_feat = x[src]
        group = jnp.clip(edge_types // NUM_REL, 0, 2)
        msg = jnp.zeros((src_feat.shape[0], D_OUT), dtype=x.dtype)
        for g in range(3):
            mask = (group == g).astype(x.dtype)[:, None]
            msg = msg + mask * (src_feat @ W[g] + b[g])
        out = jax.ops.segment_sum(msg, dst, num_segments=x.shape[0])
        deg = jax.ops.segment_sum(jnp.ones_like(dst, dtype=x.dtype), dst, num_segments=x.shape[0])
        deg = jnp.maximum(deg, 1.0)
        return jax.nn.relu(out / deg[:, None])
    edge_index = jnp.stack([src, dst])
    x = _layernorm(x + _L0_gnn_ref(x, edge_index, edge_weight, L0_gnn_W_rel, L0_gnn_b_rel, L0_gnn_W_root), axis=-1)
    x = _layernorm(x + _L1_gnn_ref(x, edge_index, edge_type_30, L1_gnn_W, L1_gnn_b), axis=-1)
    return x

_drawn_inputs = setup_inputs


def setup_inputs(seed=0):
    import zlib

    import numpy as np

    out = dict(_drawn_inputs(seed))
    spreads = {}
    factors = {'L1_gnn_b': 2.806}
    for name, (base, spread) in spreads.items():
        noise = np.random.default_rng([zlib.crc32(name.encode()), seed]).standard_normal(out[name].shape)
        drawn = base * np.exp(spread * noise) if base else spread * noise
        out[name] = jnp.asarray(drawn.astype(out[name].dtype))
    for name, factor in factors.items():
        out[name] = (out[name] * factor).astype(out[name].dtype)
    return out
```

```python
from contextlib import ExitStack

import concourse.bass as bass
from concourse import mybir

ALU = mybir.AluOpType
ACT = mybir.ActivationFunctionType
F32 = mybir.dt.float32
I32 = mybir.dt.int32

P = 128
NODES = 50000
EDGES = 25000
D = 128
LAYERS = 3
GRADES = 3
PER_GRADE = 10
EPS = 1e-5
NG = 4
NODE_TILES = -(-NODES // (P * NG)) * NG
EDGE_TILES = -(-EDGES // (P * NG)) * NG
ROWS = NODE_TILES * P
SLOTS = EDGE_TILES * P
PAD_DST = ROWS - 1
META = 4
EW = D + META


def gnn_kernel(nc, x, src, dst, dst_rows, etype, weight, w_rel, b_rel, w_root, w_typed, b_typed, out):
    h_tabs = [x] + [nc.dram_tensor(f"h{l}", (ROWS, D), F32, kind="Internal").ap() for l in (1, 2, 3)] + [out]
    agg = nc.dram_tensor("agg", (ROWS + P, EW), F32, kind="Internal").ap()
    h_tiles = [h.rearrange("(t p) d -> t p d", p=P) for h in h_tabs]
    agg_tiles = agg.rearrange("(t p) d -> t p d", p=P)

    with ExitStack() as ctx:
        def sb(name, shape, dt=F32):
            return ctx.enter_context(nc.sbuf_tensor(name, shape, dt))

        def pb(name, shape):
            return ctx.enter_context(nc.psum_tensor(name, shape, F32))

        def sem(name):
            return ctx.enter_context(nc.semaphore(name))

        src_tab = sb("src_tab", [P, EDGE_TILES], I32)
        dst_tab = sb("dst_tab", [P, EDGE_TILES], I32)
        type_tab = sb("type_tab", [P, EDGE_TILES], I32)
        weight_tab = sb("weight_tab", [P, EDGE_TILES])
        meta = sb("meta", [P, EDGE_TILES, META])
        grade = sb("grade", [P, GRADES, EDGE_TILES])
        rel_w = sb("rel_w", [P, LAYERS, D])
        root_w = sb("root_w", [P, LAYERS, D])
        typed_w = sb("typed_w", [P, GRADES, D])
        rel_b = sb("rel_b", [P, LAYERS, D])
        typed_b = sb("typed_b", [P, GRADES, D])
        ident = sb("ident", [P, P])
        earlier = sb("earlier", [P, P])
        zeros = sb("zeros", [P, EW])
        eps_col = sb("eps_col", [P, 1])
        dump_i = sb("dump_i", [P, 1], I32)
        dump_f = sb("dump_f", [P, 1])

        src_slot = sb("src_slot", [P, 1], I32)
        dst_row = sb("dst_row", [P, P], I32)
        feats = sb("feats", [P, EW])
        same = sb("same", [P, P])
        same_before = sb("same_before", [P, P])
        repeats = sb("repeats", [P, 1])
        target_f = sb("target_f", [P, 1])
        target = sb("target", [P, 1], I32)
        feats_t = sb("feats_t", [P, D])
        typed_msg = sb("typed_msg", [P, GRADES, D])
        msg = sb("msg", [P, EW])
        summed = sb("summed", [P, EW])
        h_in = sb("h_in", [P, D])
        agg_in = sb("agg_in", [P, EW])
        res_in = sb("res_in", [P, D])
        both_t = sb("both_t", [P, 2 * D])
        z = sb("z", [P, D])
        z2 = sb("z2", [P, D])
        stats = sb("stats", [P, 6])
        mean_var = sb("mean_var", [P, 2])
        std = sb("std", [P, 1])
        rstd = sb("rstd", [P, 1])
        deg = sb("deg", [P, 1])
        ps_t = pb("ps_t", [P, 2 * D])
        ps_typed = pb("ps_typed", [P, GRADES * D])
        ps_sum = pb("ps_sum", [P, EW])
        ps_out = pb("ps_out", [P, D])

        s_in = sem("s_in")
        s_const = sem("s_const")
        s_meta = sem("s_meta")
        s_zeroed = sem("s_zeroed")
        s_scatter = sem("s_scatter")
        s_turn = sem("s_turn")
        s_slot = sem("s_slot")
        s_gather = sem("s_gather")
        s_dstrow = sem("s_dstrow")
        s_same = sem("s_same")
        s_target = sem("s_target")
        s_ft = sem("s_ft")
        s_fte = sem("s_fte")
        s_typed = sem("s_typed")
        s_msg = sem("s_msg")
        s_sum = sem("s_sum")
        s_summed = sem("s_summed")
        s_node = sem("s_node")
        s_load = sem("s_load")
        s_tr = sem("s_tr")
        s_tre = sem("s_tre")
        s_prod = sem("s_prod")
        s_z = sem("s_z")
        s_std = sem("s_std")
        s_done = sem("s_done")
        s_nop = sem("s_nop")

        INPUT_LOADS = 9
        block = ctx.enter_context(nc.Block())

        def edge_loops():
            return [(l, l * EDGE_TILES) for l in range(LAYERS + 1)]

        LOADS = [2, 2, 3, 2]

        @block.sync
        def _(sp):
            for to, of in ((src_tab, src), (dst_tab, dst), (type_tab, etype), (weight_tab, weight)):
                sp.dma_start(to[:, :], of).then_inc(s_in, 16)
            sp.dma_start(rel_w[:, :, :], w_rel.rearrange("l k n -> k l n")).then_inc(s_in, 16)
            sp.dma_start(root_w[:, :, :], w_root.rearrange("l k n -> k l n")).then_inc(s_in, 16)
            sp.dma_start(typed_w[:, :, :], w_typed.rearrange("l k n -> k l n")).then_inc(s_in, 16)
            sp.dma_start(rel_b[:, :, :], b_rel.partition_broadcast(P)).then_inc(s_in, 16)
            sp.dma_start(typed_b[:, :, :], b_typed.partition_broadcast(P)).then_inc(s_in, 16)
            sp.wait_ge(s_const, 1)
            sp.dma_start(agg_tiles.rearrange("t p d -> p t d"),
                         zeros[:, :].unsqueeze(1).broadcast_to([P, NODE_TILES + 1, EW])).then_inc(s_zeroed, 16)
            loads = 0
            for l, before in edge_loops():
                with sp.Fori(0, EDGE_TILES) as t:
                    sp.wait_ge(s_turn, before + 1 + t)
                    sp.dma_start(dst_row[:, :], dst_rows[bass.ds(t, 1), :].squeeze(0).partition_broadcast(P)
                                 ).then_inc(s_dstrow, 16)
                sp.wait_ge(s_turn, before + EDGE_TILES + 1)
                with sp.Fori(0, NODE_TILES) as i:
                    sp.wait_ge(s_node, 32 * (l * NODE_TILES + 1 + i))
                    sp.dma_start(agg_in[:, :], agg_tiles[bass.ds(i, 1)].squeeze(0)).then_inc(s_load, 16)
                    if l < LAYERS:
                        sp.dma_start(h_in[:, :], h_tiles[l][bass.ds(i, 1)].squeeze(0)).then_inc(s_load, 16)
                    if l >= LAYERS - 1:
                        res = x.rearrange("(t p) d -> t p d", p=P) if l == LAYERS - 1 else h_tiles[LAYERS]
                        sp.dma_start(res_in[:, :], res[bass.ds(i, 1)].squeeze(0)).then_inc(s_load, 16)
                    sp.wait_ge(s_load, 16 * loads + 16 * LOADS[l] * (i + 1))
                    sp.dma_start(agg_tiles[bass.ds(i, 1)].squeeze(0), zeros[:, :]).then_inc(s_node, 16)
                    sp.wait_ge(s_done, l * NODE_TILES + 1 + i)
                    sp.dma_start(h_tiles[l + 1][bass.ds(i, 1)].squeeze(0), z[:, :]).then_inc(s_node, 16)
                loads += LOADS[l] * NODE_TILES
            sp.wait_ge(s_node, 32 * (NODE_TILES * (LAYERS + 1) + 1))

        @block.gpsimd
        def _(pool):
            pool.memset(zeros[:, :], 0.0).then_inc(s_const, 1)
            pool.memset(ident[:, :], 0.0).then_inc(s_const, 1)
            pool.memset(earlier[:, :], 1.0).then_inc(s_const, 1)
            pool.memset(eps_col[:, :], EPS).then_inc(s_const, 1)
            pool.wait_ge(s_const, 4)
            pool.affine_select(out=ident[:, :], in_=ident[:, :], compare_op=ALU.not_equal, fill=1.0, base=0,
                               pattern=[[-1, P]], channel_multiplier=1).then_inc(s_const, 1)
            pool.affine_select(out=earlier[:, :], in_=earlier[:, :], compare_op=ALU.is_gt, fill=0.0, base=0,
                               pattern=[[-1, P]], channel_multiplier=1).then_inc(s_const, 1)
            pool.iota(dump_i[:, :], pattern=[[0, 1]], base=ROWS, channel_multiplier=1).then_inc(s_const, 1)
            pool.sem_inc(s_node, 32)
            pool.wait_ge(s_zeroed, 16)
            pool.sem_inc(s_turn, 1)
            pool.wait_ge(s_in, 16 * INPUT_LOADS)
            pool.wait_ge(s_meta, 1)
            for l, before in edge_loops():
                if l:
                    pool.wait_ge(s_node, 32 * (l * NODE_TILES + 1))
                with pool.Fori(0, EDGE_TILES) as t:
                    pool.wait_ge(s_turn, before + 1 + t)
                    pool.tensor_copy(src_slot[:, :], src_tab[:, bass.ds(t, 1)]).then_inc(s_slot, 1)
                    pool.wait_ge(s_slot, before + 1 + t)
                    pool.sem_inc(s_nop, 1)
                    pool.indirect_dma_start(out=feats[:, 0:D], out_offset=None, in_=h_tabs[l][:, :],
                                            in_offset=bass.IndirectOffsetOnAxis(ap=src_slot[:, 0:1], axis=0)
                                            ).then_inc(s_gather, 16)
                    pool.wait_ge(s_target, before + 1 + t)
                    pool.wait_ge(s_summed, before + 1 + t)
                    pool.sem_inc(s_nop, 1)
                    pool.indirect_dma_start(out=agg[:, :], in_=summed[:, :], in_offset=None,
                                            out_offset=bass.IndirectOffsetOnAxis(ap=target[:, 0:1], axis=0),
                                            compute_op=ALU.add).then_inc(s_scatter, 16)
                    pool.wait_ge(s_scatter, 16 * (before + 1 + t))
                    pool.sem_inc(s_turn, 1)

        @block.vector
        def _(dve):
            dve.wait_ge(s_in, 16 * INPUT_LOADS)
            dve.wait_ge(s_const, 7)
            dve.memset(meta[:, :, 0:1], 1.0)
            dve.tensor_copy(meta[:, :, 1], dst_tab[:, :])
            dve.tensor_copy(meta[:, :, 2], weight_tab[:, :])
            dve.tensor_copy(meta[:, :, 3], type_tab[:, :])
            dve.tensor_copy(dump_f[:, :], dump_i[:, :])
            dve.tensor_scalar(grade[:, 0, :], type_tab[:, :], float(PER_GRADE), None, ALU.is_lt)
            dve.tensor_scalar(grade[:, 2, :], type_tab[:, :], float(2 * PER_GRADE), None, ALU.is_ge)
            dve.drain()
            dve.tensor_tensor(grade[:, 1, :], grade[:, 0, :], grade[:, 2, :], ALU.add)
            dve.drain()
            dve.tensor_scalar(grade[:, 1, :], grade[:, 1, :], -1.0, 1.0, ALU.mult, ALU.add)
            dve.drain().then_inc(s_meta, 1)
            for l, before in edge_loops():
                with dve.Fori(0, EDGE_TILES) as t:
                    dve.wait_ge(s_turn, before + 1 + t)
                    dve.wait_ge(s_dstrow, 16 * (before + 1 + t))
                    dst_col = meta[:, bass.ds(t, 1), 1]
                    dve.scalar_tensor_tensor(out=same_before[:, :], in0=dst_row[:, :], scalar=dst_col,
                                             in1=earlier[:, :], op0=ALU.is_equal, op1=ALU.mult,
                                             accum_out=repeats[:, :])
                    if l < LAYERS:
                        dve.tensor_scalar(same[:, :], dst_row[:, :], dst_col, meta[:, bass.ds(t, 1), 2],
                                          ALU.is_equal, ALU.mult).then_inc(s_same, 1)
                    else:
                        dve.tensor_scalar(same[:, :], dst_row[:, :], dst_col, None,
                                          ALU.is_equal).then_inc(s_same, 1)
                    dve.drain()
                    dve.tensor_scalar(repeats[:, :], repeats[:, :], 0.5, None, ALU.is_gt)
                    dve.tensor_tensor(target_f[:, :], dump_f[:, :], dst_col, ALU.subtract)
                    dve.drain()
                    dve.tensor_tensor(target_f[:, :], target_f[:, :], repeats[:, :], ALU.mult)
                    dve.drain()
                    dve.tensor_tensor(target[:, :], target_f[:, :], dst_col, ALU.add).then_inc(s_target, 1)
                    if l < LAYERS:
                        dve.tensor_copy(feats[:, D:EW], meta[:, bass.ds(t, 1), :].squeeze(1)).then_inc(s_msg, 1)
                    else:
                        dve.wait_ge(s_typed, t + 1)
                        dve.tensor_tensor(typed_msg[:, :, :].rearrange("p a b -> p (a b)"), ps_typed[:, :],
                                          typed_b[:, :, :].rearrange("p a b -> p (a b)"), ALU.add)
                        dve.drain()
                        dve.tensor_scalar(msg[:, 0:D], typed_msg[:, 0, :], grade[:, 0, bass.ds(t, 1)], None, ALU.mult)
                        for g in (1, 2):
                            dve.drain()
                            dve.scalar_tensor_tensor(out=msg[:, 0:D], in0=typed_msg[:, g, :],
                                                     scalar=grade[:, g, bass.ds(t, 1)], in1=msg[:, 0:D],
                                                     op0=ALU.mult, op1=ALU.add)
                        dve.tensor_copy(msg[:, D:EW], meta[:, bass.ds(t, 1), :].squeeze(1))
                        dve.drain().then_inc(s_msg, 1)
                loads = NODE_TILES * sum(LOADS[:l])
                normed = max(0, l - LAYERS + 1) * NODE_TILES
                with dve.Fori(0, NODE_TILES) as i:
                    if l < LAYERS:
                        dve.wait_ge(s_prod, l * NODE_TILES + 1 + i)
                        dve.tensor_tensor(z2[:, :], ps_out[:, :], rel_b[:, l, :], ALU.add)
                        dve.drain()
                        if l < LAYERS - 1:
                            dve.tensor_scalar(z[:, :], z2[:, :], 0.0, None, ALU.max).then_inc(s_done, 1)
                            continue
                        dve.tensor_tensor(z2[:, :], z2[:, :], res_in[:, :], ALU.add)
                    else:
                        dve.wait_ge(s_load, 16 * loads + 16 * LOADS[l] * (i + 1))
                        dve.tensor_scalar(deg[:, :], agg_in[:, D:D + 1], 1.0, None, ALU.max)
                        dve.drain()
                        dve.reciprocal(deg[:, :], deg[:, :])
                        dve.drain()
                        dve.tensor_scalar(z2[:, :], agg_in[:, 0:D], deg[:, 0:1], 0.0, ALU.mult, ALU.max)
                        dve.drain()
                        dve.tensor_tensor(z2[:, :], z2[:, :], res_in[:, :], ALU.add)
                    dve.drain()
                    dve.bn_stats(stats[:, :], z2[:, :])
                    dve.drain()
                    dve.bn_aggr(mean_var[:, :], stats[:, :])
                    dve.drain().then_inc(s_z, 1)
                    dve.wait_ge(s_std, normed + 1 + i)
                    dve.reciprocal(rstd[:, :], std[:, :])
                    dve.drain()
                    dve.tensor_scalar(z[:, :], z2[:, :], mean_var[:, 0:1], rstd[:, 0:1], ALU.subtract,
                                      ALU.mult).then_inc(s_done, 1)

        @block.tensor
        def _(pe):
            pe.wait_ge(s_const, 7)
            pe.wait_ge(s_in, 16 * INPUT_LOADS)
            for l, before in edge_loops():
                with pe.Fori(0, EDGE_TILES) as t:
                    pe.wait_ge(s_gather, 16 * (before + 1 + t))
                    if l == LAYERS:
                        pe.transpose(ps_t[:, 0:D], feats[:, 0:D], ident[:, :]).then_inc(s_ft, 1)
                        pe.wait_ge(s_fte, t + 1)
                        pe.matmul(ps_typed[:, :], feats_t[:, :], typed_w[:, :, :].rearrange("p a b -> p (a b)"),
                                  start=True, stop=True).then_inc(s_typed, 1)
                    pe.wait_ge(s_same, before + 1 + t)
                    pe.wait_ge(s_msg, before + 1 + t)
                    pe.matmul(ps_sum[:, :], same[:, :], (msg if l == LAYERS else feats)[:, :],
                              start=True, stop=True).then_inc(s_sum, 1)
                if l == LAYERS:
                    continue
                loads = NODE_TILES * sum(LOADS[:l])
                with pe.Fori(0, NODE_TILES) as i:
                    pe.wait_ge(s_load, 16 * loads + 16 * LOADS[l] * (i + 1))
                    pe.transpose(ps_t[:, 0:D], h_in[:, :], ident[:, :])
                    pe.transpose(ps_t[:, D:2 * D], agg_in[:, 0:D], ident[:, :]).then_inc(s_tr, 1)
                    pe.wait_ge(s_tre, l * NODE_TILES + 1 + i)
                    pe.matmul(ps_out[:, :], both_t[:, 0:D], root_w[:, l, :], start=True, stop=False)
                    pe.matmul(ps_out[:, :], both_t[:, D:2 * D], rel_w[:, l, :],
                              start=False, stop=True).then_inc(s_prod, 1)

        @block.scalar
        def _(act):
            for l, before in edge_loops():
                with act.Fori(0, EDGE_TILES) as t:
                    if l == LAYERS:
                        act.wait_ge(s_ft, t + 1)
                        act.activation(feats_t[:, :], ps_t[:, 0:D], ACT.Copy).then_inc(s_fte, 1)
                    act.wait_ge(s_sum, before + 1 + t)
                    act.activation(summed[:, :], ps_sum[:, :], ACT.Copy).then_inc(s_summed, 1)
                with act.Fori(0, NODE_TILES) as i:
                    if l < LAYERS:
                        act.wait_ge(s_tr, l * NODE_TILES + 1 + i)
                        act.activation(both_t[:, :], ps_t[:, :], ACT.Copy).then_inc(s_tre, 1)
                    if l >= LAYERS - 1:
                        act.wait_ge(s_z, (l - LAYERS + 1) * NODE_TILES + 1 + i)
                        act.activation(std[:, :], mean_var[:, 1:2], ACT.Sqrt,
                                       bias=eps_col[:, 0:1]).then_inc(s_std, 1)


def kernel(**inputs):
    import numpy as _np
    import concourse.bacc as _bacc
    from concourse import mybir as _mybir
    from concourse.bass_utils import run_bass_kernel_spmd as _run

    a = {k: _np.asarray(v) for k, v in inputs.items()}

    def padded(v, rows, fill=0):
        tail = _np.full((rows - v.shape[0],) + v.shape[1:], fill, v.dtype)
        return _np.concatenate([v, tail])

    def by_tile(v, fill=0):
        return _np.ascontiguousarray(padded(v, SLOTS, fill).reshape(EDGE_TILES, P).T)

    arrays = {
        "in_x": padded(a["x"], ROWS),
        "in_src": by_tile(a["src"]),
        "in_dst": by_tile(a["dst"], PAD_DST),
        "in_dst_rows": padded(a["dst"], SLOTS, PAD_DST).reshape(EDGE_TILES, P),
        "in_type": by_tile(a["edge_type_30"]),
        "in_weight": by_tile(a["edge_weight"]),
        "in_w_rel": a["L0_gnn_W_rel"], "in_b_rel": a["L0_gnn_b_rel"], "in_w_root": a["L0_gnn_W_root"],
        "in_w_typed": a["L1_gnn_W"], "in_b_typed": a["L1_gnn_b"],
    }
    nc = _bacc.Bacc("TRN2", target_bir_lowering=False, num_devices=1)
    args = [nc.dram_tensor(n, v.shape, _mybir.dt.from_np(v.dtype), kind="ExternalInput").ap()
            for n, v in arrays.items()]
    args.append(nc.dram_tensor("out_x", (ROWS, D), _mybir.dt.float32, kind="ExternalOutput").ap())
    gnn_kernel(nc, *args)
    r = _run(nc, [arrays], core_ids=[0])
    return r.results[0]["out_x"][:NODES]
```

```python
from contextlib import ExitStack

import concourse.bass as bass
from concourse import mybir

ALU = mybir.AluOpType
ACT = mybir.ActivationFunctionType
F32 = mybir.dt.float32
I32 = mybir.dt.int32

P = 128
NODES = 50000
EDGES = 25000
D = 128
LAYERS = 3
GRADES = 3
PER_GRADE = 10
EPS = 1e-5
NG = 4
NODE_TILES = -(-NODES // (P * NG)) * NG
EDGE_TILES = -(-EDGES // (P * NG)) * NG
ROWS = NODE_TILES * P
SLOTS = EDGE_TILES * P
PAD_DST = ROWS - 1
META = 4
EW = D + META

STEPS = NODE_TILES // (2 * NG)
EDGE_GROUPS = EDGE_TILES // NG
BODY = 4
LEAD = 3
WIN = 112
START_MASK = 0x7FFF
GD = NG * D
NGP = NODE_TILES // NG
CREDIT = 4
LOOPED = (STEPS - LEAD - 2) // BODY
RES_BODIES = 6
RES_STEPS = RES_BODIES * BODY + 1
RES_GROUPS = 2 * RES_STEPS


def nth(n, back=0):
    return n + 1 - back + CREDIT


class At:

    def __init__(self, i, c, per):
        self.i, self.c, self.per = i, c, per
        self.n = i * per + c

    def plus(self, k):
        return At(self.i, self.c + k, self.per)

    def slot(self, ring):
        return self.c % ring

    def uses(self, ring, total, layer):
        before = layer * len(range(self.c % ring, total, ring))
        return self.i * (self.per // ring) + self.c // ring + 1 + before


def count(slot, ring, to, since=0):
    return len([n for n in range(since, to) if n % ring == slot])


def stores(layers, slot):
    return layers * count(slot, 2, STEPS)


def spills(layers, slot):
    return min(layers, LAYERS - 1) * count(slot, 2, NGP, RES_GROUPS)


def spills_before(l, g, kept_here):
    if l == LAYERS - 1 or kept_here:
        return CREDIT + spills(l, g.slot(2))
    return CREDIT + spills(l, g.slot(2)) + g.uses(2, NGP, 0) - 1 - count(g.slot(2), 2, RES_GROUPS)


def feat_uses(l, g):
    if l == 0:
        return g.uses(4, NGP, 0)
    slot = g.slot(4)
    return (count(slot, 4, NGP) + (l - 1) * count(slot, 4, NGP, RES_GROUPS)
            + g.uses(4, NGP, 0) - count(slot, 4, RES_GROUPS))


def resid_uses(l, m):
    if l < LAYERS:
        return m.uses(2, STEPS, 0)
    return count(m.slot(2), 2, STEPS) + m.uses(2, STEPS, 0) - count(m.slot(2), 2, RES_STEPS)


def walk(engine, step):
    step(At(0, 0, BODY), True, True, first=True)
    with engine.Fori(0, RES_BODIES) as i:
        for c in range(BODY):
            step(At(i, 1 + c, BODY), True, True)
    step(At(RES_BODIES, 1, BODY), False, True)
    with engine.Fori(RES_BODIES, LOOPED) as i:
        for c in range(BODY):
            step(At(i, 2 + c, BODY), False, False)
    for m in range(LOOPED * BODY + 2, STEPS):
        step(At(m // BODY, m % BODY, BODY), False, False, last=m == STEPS - 1)


def gnn_kernel(nc, x, x_t, src, dst, dst_rows, etype, weight, w_rel, b_rel, w_root, w_typed, b_typed, out):
    h_tabs = [x] + [nc.dram_tensor(f"h{l}", (ROWS, D), F32, kind="Internal").ap() for l in (1, 2, 3)] + [out]
    agg = nc.dram_tensor("agg", (ROWS + P, EW), F32, kind="Internal").ap()
    h_tiles = [h.rearrange("(t p) d -> t p d", p=P) for h in h_tabs]
    h_steps = [h.rearrange("(s t p) d -> s p t d", p=P, t=2 * NG) for h in h_tabs]
    edge_rows = nc.dram_tensor("edge_rows", (START_MASK + 1 + WIN, EW), F32, kind="Internal").ap()
    edge_groups = edge_rows[0:SLOTS, :].rearrange("(g t p) d -> g p t d", p=P, t=NG)
    spill = nc.dram_tensor("spill", (NGP, D, GD), F32, kind="Internal").ap()
    starts_dram = nc.dram_tensor("starts_dram", (NGP, 2), I32, kind="Internal").ap()
    agg_tiles = agg.rearrange("(t p) d -> t p d", p=P)

    with ExitStack() as ctx:
        def sb(name, shape, dt=F32):
            return ctx.enter_context(nc.sbuf_tensor(name, shape, dt))

        def pb(name, shape):
            return ctx.enter_context(nc.psum_tensor(name, shape, F32))

        def sem(name):
            return ctx.enter_context(nc.semaphore(name))

        src_tab = sb("src_tab", [P, EDGE_TILES], I32)
        dst_tab = sb("dst_tab", [P, EDGE_TILES], I32)
        type_tab = sb("type_tab", [P, EDGE_TILES], I32)
        weight_tab = sb("weight_tab", [P, EDGE_TILES])
        meta = sb("meta", [P, EDGE_TILES, META])
        grade = sb("grade", [P, GRADES, EDGE_TILES])
        rel_w = sb("rel_w", [P, LAYERS, D])
        root_w = sb("root_w", [P, LAYERS, D])
        typed_w = sb("typed_w", [P, GRADES, D])
        rel_b = sb("rel_b", [P, LAYERS, D])
        typed_b = sb("typed_b", [P, GRADES, D])
        ident = sb("ident", [P, P])
        earlier = sb("earlier", [P, P])
        zeros = sb("zeros", [P, EW])
        eps_col = sb("eps_col", [P, 1])
        dump_i = sb("dump_i", [P, 1], I32)
        dump_f = sb("dump_f", [P, 1])

        rel_bt = sb("rel_bt", [P, LAYERS])
        iota_row = sb("iota_row", [P, P])
        tile_base = sb("tile_base", [P, NODE_TILES])
        thresh_i = sb("thresh_i", [P, NG + 1], I32)
        thresh = sb("thresh", [P, NG + 1])
        pick_last = sb("pick_last", [P, P])
        ones_col = sb("ones_col", [P, 1])
        scan = sb("scan", [P, EDGE_TILES])
        found_tile = sb("found_tile", [P, NG + 1])
        found_tile_i = sb("found_tile_i", [P, NG + 1], I32)
        found_rows = sb("found_rows", [P, NG + 1, P], I32)
        found_in = sb("found_in", [P, NG + 1])
        starts = sb("starts", [P, NG + 1])
        starts_i = sb("starts_i", [P, NG], I32)
        starts_hi = sb("starts_hi", [P, 2], I32)
        starts_word = sb("starts_word", [P, 2], I32)
        pace_i = sb("pace_i", [P, 1], I32)
        pace = sb("pace", [P, 1])
        order = sb("order", [P, 2, EDGE_TILES], I32)
        bad = sb("bad", [P, 3])
        bad_scr = sb("bad_scr", [P, NG])
        bad_sum = sb("bad_sum", [P, 1])
        flag = sb("flag", [1, 1], I32)
        words = sb("words", [1, 2 * NGP], I32)
        kept = sb("kept", [P, RES_GROUPS * GD])
        src_ring = sb("src_ring", [P, 4, NG], I32)
        gather_ring = sb("gather_ring", [P, 4, NG, D])
        edge_t = sb("edge_t", [P, 2, GD])
        edge_out = sb("edge_out", [P, 4, NG, EW])
        typed_ring = sb("typed_ring", [P, GRADES * D])
        win = sb("win", [P, 4, NG, EW])
        feat_t = sb("feat_t", [P, 4, GD])
        rel_dst = sb("rel_dst", [P, 2, NG])
        place = sb("place", [P, 4, NG, P])
        next_t = sb("next_t", [P, 2, GD])
        rows = sb("rows", [P, 2, 2 * NG, D])
        resid = sb("resid", [P, 2, 2 * NG, D])
        pre = sb("pre", [P, 2, NG, D])
        ln_stats = sb("ln_stats", [P, 2, NG, 6])
        ln_mv = sb("ln_mv", [P, 2, NG, 2])
        ln_std = sb("ln_std", [P, 2, NG])
        ln_rstd = sb("ln_rstd", [P, 2, NG])
        inv_deg = sb("inv_deg", [P, 2, NG])
        src_slot = sb("src_slot", [P, 1], I32)
        dst_row = sb("dst_row", [P, P], I32)
        feats = sb("feats", [P, EW])
        same = sb("same", [P, P])
        same_before = sb("same_before", [P, P])
        repeats = sb("repeats", [P, 1])
        target_f = sb("target_f", [P, 1])
        target = sb("target", [P, 1], I32)
        feats_t = sb("feats_t", [P, D])
        typed_msg = sb("typed_msg", [P, GRADES, D])
        msg = sb("msg", [P, EW])
        summed = sb("summed", [P, EW])
        h_in = sb("h_in", [P, D])
        agg_in = sb("agg_in", [P, EW])
        res_in = sb("res_in", [P, D])
        both_t = sb("both_t", [P, 2 * D])
        z = sb("z", [P, D])
        z2 = sb("z2", [P, D])
        stats = sb("stats", [P, 6])
        mean_var = sb("mean_var", [P, 2])
        std = sb("std", [P, 1])
        rstd = sb("rstd", [P, 1])
        deg = sb("deg", [P, 1])
        ps_edge_t = [pb(f"ps_edge_t{b}", [P, GD]) for b in range(2)]
        ps_edge_out = [pb(f"ps_edge_out{b}", [P, GD]) for b in range(2)]
        ps_node = [pb(f"ps_node{b}", [P, GD]) for b in range(2)]
        ps_rows = [pb(f"ps_rows{b}", [P, GD]) for b in range(2)]
        ps_t = ps_edge_t[0][:, 0:2 * D]
        ps_typed = ps_edge_out[0][:, 0:GRADES * D]
        ps_sum = ps_node[0][:, 0:EW]
        ps_out = ps_rows[0][:, 0:D]

        s_in = sem("s_in")
        s_const = sem("s_const")
        s_meta = sem("s_meta")
        s_zeroed = sem("s_zeroed")
        s_scatter = sem("s_scatter")
        s_turn = sem("s_turn")
        s_slot = sem("s_slot")
        s_gather = sem("s_gather")
        s_dstrow = sem("s_dstrow")
        s_same = sem("s_same")
        s_target = sem("s_target")
        s_ft = sem("s_ft")
        s_fte = sem("s_fte")
        s_typed = sem("s_typed")
        s_msg = sem("s_msg")
        s_sum = sem("s_sum")
        s_summed = sem("s_summed")
        s_node = sem("s_node")
        s_load = sem("s_load")
        s_tr = sem("s_tr")
        s_tre = sem("s_tre")
        s_prod = sem("s_prod")
        s_z = sem("s_z")
        s_std = sem("s_std")
        s_done = sem("s_done")
        s_nop = sem("s_nop")

        s_flag = sem("s_flag")
        s_pre = sem("s_pre")
        s_find = sem("s_find")
        s_found = sem("s_found")
        s_words = sem("s_words")
        s_order = sem("s_order")
        s_src = sem("s_src")
        s_gathered = [sem(f"s_gathered{b}") for b in range(4)]
        s_edge_t = sem("s_edge_t")
        s_edge_te = sem("s_edge_te")
        s_edge_p = sem("s_edge_p")
        s_typed_p = sem("s_typed_p")
        s_typed_e = sem("s_typed_e")
        s_edge_out = sem("s_edge_out")
        s_edge_meta = sem("s_edge_meta")
        s_edge_st = sem("s_edge_st")
        s_win = [sem(f"s_win{b}") for b in range(4)]
        s_feat = [sem(f"s_feat{b}") for b in range(4)]
        s_resid = [sem(f"s_resid{b}") for b in range(2)]
        s_rel = sem("s_rel")
        s_place = sem("s_place")
        s_node_p = sem("s_node_p")
        s_next = sem("s_next")
        s_spill = [sem(f"s_spill{b}") for b in range(2)]
        s_back = sem("s_back")
        s_rows = sem("s_rows")
        s_store = [sem(f"s_store{b}") for b in range(2)]
        s_dve = sem("s_dve")
        s_var = sem("s_var")
        s_lnstd = sem("s_lnstd")
        s_deg = sem("s_deg")
        s_degmax = sem("s_degmax")
        s_lnsum = sem("s_lnsum")
        s_ln = sem("s_ln")
        s_rstd = sem("s_rstd")
        s_kept = sem("s_kept")
        s_idle = sem("s_idle")

        INPUT_LOADS = 10
        block = ctx.enter_context(nc.Block())

        def edge_loops():
            return [(l, l * EDGE_TILES) for l in range(LAYERS + 1)]

        LOADS = [2, 2, 3, 2]

        @block.sync
        def _(sp):
            for to, of in ((src_tab, src), (dst_tab, dst), (type_tab, etype), (weight_tab, weight)):
                sp.dma_start(to[:, :], of).then_inc(s_in, 16)
            sp.dma_start(rel_w[:, :, :], w_rel.rearrange("l k n -> k l n")).then_inc(s_in, 16)
            sp.dma_start(root_w[:, :, :], w_root.rearrange("l k n -> k l n")).then_inc(s_in, 16)
            sp.dma_start(typed_w[:, :, :], w_typed.rearrange("l k n -> k l n")).then_inc(s_in, 16)
            sp.dma_start(rel_b[:, :, :], b_rel.partition_broadcast(P)).then_inc(s_in, 16)
            sp.dma_start(typed_b[:, :, :], b_typed.partition_broadcast(P)).then_inc(s_in, 16)
            sp.dma_start(rel_bt[:, :], b_rel.rearrange("l d -> d l"), allow_slow_non_contiguous=True
                         ).then_inc(s_in, 16)
            flat = dst_rows.rearrange("t p -> (t p)")
            sp.dma_start(order[:, 0, :], flat[0:SLOTS].rearrange("(p t) -> p t", p=P)).then_inc(s_order, 16)
            sp.dma_start(order[:, 1, :], flat[1:SLOTS + 1].rearrange("(p t) -> p t", p=P)).then_inc(s_order, 16)
            sp.wait_ge(s_find, 3)
            sp.dma_start(starts_dram[:, :], starts_word[0:NGP, :]).then_inc(s_words, 16)
            sp.wait_ge(s_words, 16)
            sp.dma_start(words[:, :], starts_dram.rearrange("(o g) w -> o (g w)", o=1)).then_inc(s_words, 16)

            def general():
                sp.wait_ge(s_const, 1)
                sp.dma_start(agg_tiles.rearrange("t p d -> p t d"),
                             zeros[:, :].unsqueeze(1).broadcast_to([P, NODE_TILES + 1, EW])).then_inc(s_zeroed, 16)
                loads = 0
                for l, before in edge_loops():
                    with sp.Fori(0, EDGE_TILES) as t:
                        sp.wait_ge(s_turn, before + 1 + t)
                        sp.dma_start(dst_row[:, :], dst_rows[bass.ds(t, 1), :].squeeze(0).partition_broadcast(P)
                                     ).then_inc(s_dstrow, 16)
                    sp.wait_ge(s_turn, before + EDGE_TILES + 1)
                    with sp.Fori(0, NODE_TILES) as i:
                        sp.wait_ge(s_node, 32 * (l * NODE_TILES + 1 + i))
                        sp.dma_start(agg_in[:, :], agg_tiles[bass.ds(i, 1)].squeeze(0)).then_inc(s_load, 16)
                        if l < LAYERS:
                            sp.dma_start(h_in[:, :], h_tiles[l][bass.ds(i, 1)].squeeze(0)).then_inc(s_load, 16)
                        if l >= LAYERS - 1:
                            res = x.rearrange("(t p) d -> t p d", p=P) if l == LAYERS - 1 else h_tiles[LAYERS]
                            sp.dma_start(res_in[:, :], res[bass.ds(i, 1)].squeeze(0)).then_inc(s_load, 16)
                        sp.wait_ge(s_load, 16 * loads + 16 * LOADS[l] * (i + 1))
                        sp.dma_start(agg_tiles[bass.ds(i, 1)].squeeze(0), zeros[:, :]).then_inc(s_node, 16)
                        sp.wait_ge(s_done, l * NODE_TILES + 1 + i)
                        sp.dma_start(h_tiles[l + 1][bass.ds(i, 1)].squeeze(0), z[:, :]).then_inc(s_node, 16)
                    loads += LOADS[l] * NODE_TILES
                sp.wait_ge(s_node, 32 * (NODE_TILES * (LAYERS + 1) + 1))

            def fast():
                sp.wait_ge(s_words, 32)

                def write_edges(l, k):
                    sp.wait_ge(s_edge_out, nth(l * EDGE_GROUPS + k.n))
                    sp.wait_ge(s_edge_meta, nth(l * EDGE_GROUPS + k.n))
                    sp.wait_ge(s_edge_st, 16 * nth(l * EDGE_GROUPS + k.n, 1))
                    sp.dma_start(edge_groups[bass.ds(k.n, 1)].squeeze(0), edge_out[:, k.slot(4), :, :]
                                 ).then_inc(s_edge_st, 16)

                def load_group(l, g, kept_here):
                    sp.wait_ge(s_node_p, nth(l * NGP + g.n, 4))
                    lo = [sp.value_load(words[0:1, bass.ds(2 * g.n + w, 1)]) for w in range(2)]
                    for w in range(2):
                        for half, at in enumerate((lo[w] & START_MASK, (lo[w] >> 16) & START_MASK)):
                            sp.dma_start(win[0:WIN, g.slot(4), 2 * w + half, :], edge_rows[bass.ds(at, WIN), :]
                                         ).then_inc(s_win[g.slot(4)], 16)
                    if l == 0 or (l < LAYERS and not kept_here):
                        of = x_t if l == 0 else spill
                        sp.dma_start(feat_t[:, g.slot(4), :], of[bass.ds(g.n, 1)].squeeze(0)
                                     ).then_inc(s_feat[g.slot(4)], 16)

                def load_step(l, m, kept_here):
                    written = m.n + LEAD - 1 if not isinstance(m.n, int) else min(m.n + LEAD - 1, EDGE_GROUPS)
                    sp.wait_ge(s_edge_st, 16 * (CREDIT + l * EDGE_GROUPS + written))
                    sp.sem_inc(s_idle, 1)
                    for b in range(2):
                        load_group(l, At(m.i, 2 * m.c + b, 2 * m.per), kept_here)
                    if l == LAYERS - 1 or (l == LAYERS and not kept_here):
                        sp.wait_ge(s_rows, nth(l * NGP + 2 * m.n + 1, 4))
                        of = h_steps[0] if l < LAYERS else h_steps[LAYERS]
                        sp.dma_start(resid[:, m.slot(2), :, :], of[bass.ds(m.n, 1)].squeeze(0)
                                     ).then_inc(s_resid[m.slot(2)], 16)

                for l in range(LAYERS + 1):
                    if l:
                        for b in range(2):
                            sp.wait_ge(s_store[b], 16 * (CREDIT + stores(l, b)))
                            sp.wait_ge(s_spill[b], 16 * (CREDIT + spills(l, b)))
                        for b in range(4):
                            sp.wait_ge(s_win[b], 64 * l * len(range(b, NGP, 4)))
                    for k in range(LEAD - 1):
                        write_edges(l, At(0, k, BODY))

                    def step(m, kept_here, kept_before, first=False, last=False):
                        load_step(l, m, kept_here)
                        if not (isinstance(m.n, int) and m.n + LEAD - 1 >= EDGE_GROUPS):
                            write_edges(l, m.plus(LEAD - 1))

                    walk(sp, step)
                for b in range(2):
                    sp.wait_ge(s_store[b], 16 * (CREDIT + stores(LAYERS + 1, b)))

            sp.wait_ge(s_flag, 1)
            general_needed = sp.value_load(flag[0:1, 0:1], min_val=0, max_val=1)
            with sp.If(general_needed != 0):
                general()
            with sp.Else():
                fast()

        @block.gpsimd
        def _(pool):
            pool.memset(zeros[:, :], 0.0).then_inc(s_const, 1)
            pool.memset(ident[:, :], 0.0).then_inc(s_const, 1)
            pool.memset(earlier[:, :], 1.0).then_inc(s_const, 1)
            pool.memset(eps_col[:, :], EPS).then_inc(s_const, 1)
            pool.wait_ge(s_const, 4)
            pool.affine_select(out=ident[:, :], in_=ident[:, :], compare_op=ALU.not_equal, fill=1.0, base=0,
                               pattern=[[-1, P]], channel_multiplier=1).then_inc(s_const, 1)
            pool.affine_select(out=earlier[:, :], in_=earlier[:, :], compare_op=ALU.is_gt, fill=0.0, base=0,
                               pattern=[[-1, P]], channel_multiplier=1).then_inc(s_const, 1)
            pool.iota(dump_i[:, :], pattern=[[0, 1]], base=ROWS, channel_multiplier=1).then_inc(s_const, 1)

            pool.iota(iota_row[:, :], pattern=[[1, P]], base=0, channel_multiplier=0,
                      allow_small_or_imprecise_dtypes=True).then_inc(s_const, 1)
            pool.iota(tile_base[:, :], pattern=[[P, NODE_TILES]], base=0, channel_multiplier=0,
                      allow_small_or_imprecise_dtypes=True).then_inc(s_const, 1)
            pool.iota(thresh_i[:, :], pattern=[[P, NG + 1]], base=0, channel_multiplier=GD).then_inc(s_const, 1)
            pool.iota(pace_i[:, :], pattern=[[0, 1]], base=(LEAD - 1) * GD - GD // 2,
                      channel_multiplier=GD // 2).then_inc(s_const, 1)
            pool.memset(pick_last[:, :], 1.0).then_inc(s_const, 1)
            pool.memset(ones_col[:, :], 1.0).then_inc(s_const, 1)
            pool.wait_ge(s_const, 13)
            pool.affine_select(out=pick_last[:, :], in_=pick_last[:, :], compare_op=ALU.is_ge, fill=0.0,
                               base=1 - P, pattern=[[0, P]], channel_multiplier=1).then_inc(s_const, 1)
            for ring in (s_edge_te, s_edge_out, s_edge_meta, s_node_p, s_next, s_back, s_rows, s_place, s_deg):
                pool.sem_inc(ring, CREDIT)
            for ring in (s_edge_st, *s_store, *s_spill):
                pool.sem_inc(ring, 16 * CREDIT)
            pool.wait_ge(s_in, 16 * INPUT_LOADS)
            pool.wait_ge(s_meta, 1)
            pool.wait_ge(s_find, 1)
            for c in range(NG + 1):
                pool.indirect_dma_start(out=found_rows[0:NGP, c, :], out_offset=None, in_=dst_rows[:, :],
                                        in_offset=bass.IndirectOffsetOnAxis(ap=found_tile_i[0:NGP, c:c + 1], axis=0)
                                        ).then_inc(s_found, 16)

            def general():
                pool.sem_inc(s_node, 32)
                pool.wait_ge(s_zeroed, 16)
                pool.sem_inc(s_turn, 1)
                for l, before in edge_loops():
                    if l:
                        pool.wait_ge(s_node, 32 * (l * NODE_TILES + 1))
                    with pool.Fori(0, EDGE_TILES) as t:
                        pool.wait_ge(s_turn, before + 1 + t)
                        pool.tensor_copy(src_slot[:, :], src_tab[:, bass.ds(t, 1)]).then_inc(s_slot, 1)
                        pool.wait_ge(s_slot, before + 1 + t)
                        pool.sem_inc(s_nop, 1)
                        pool.indirect_dma_start(out=feats[:, 0:D], out_offset=None, in_=h_tabs[l][:, :],
                                                in_offset=bass.IndirectOffsetOnAxis(ap=src_slot[:, 0:1], axis=0)
                                                ).then_inc(s_gather, 16)
                        pool.wait_ge(s_target, before + 1 + t)
                        pool.wait_ge(s_summed, before + 1 + t)
                        pool.sem_inc(s_nop, 1)
                        pool.indirect_dma_start(out=agg[:, :], in_=summed[:, :], in_offset=None,
                                                out_offset=bass.IndirectOffsetOnAxis(ap=target[:, 0:1], axis=0),
                                                compute_op=ALU.add).then_inc(s_scatter, 16)
                        pool.wait_ge(s_scatter, 16 * (before + 1 + t))
                        pool.sem_inc(s_turn, 1)

            def fast():
                def gather(l, k):
                    n = l * EDGE_GROUPS + k.n
                    pool.wait_ge(s_edge_te, nth(n, 4))
                    pool.tensor_copy(src_ring[:, k.slot(4), :], src_tab[:, bass.ds(NG * k.n, NG)]).then_inc(s_src, 1)
                    pool.wait_ge(s_src, n + 1)
                    pool.sem_inc(s_idle, 1)
                    for j in range(NG):
                        pool.indirect_dma_start(
                            out=gather_ring[:, k.slot(4), j, :], out_offset=None, in_=h_tabs[l][:, :],
                            in_offset=bass.IndirectOffsetOnAxis(ap=src_ring[:, k.slot(4), j:j + 1], axis=0)
                        ).then_inc(s_gathered[k.slot(4)], 16)
                    pool.wait_ge(s_edge_st, 16 * nth(n, 4))
                    pool.tensor_copy(edge_out[:, k.slot(4), :, D:EW], meta[:, bass.ds(NG * k.n, NG), :]
                                     ).then_inc(s_edge_meta, 1)

                for l in range(LAYERS + 1):
                    if l:
                        for b in range(2):
                            pool.wait_ge(s_store[b], 16 * (CREDIT + stores(l, b)))
                    with pool.Fori(0, EDGE_GROUPS // BODY) as i:
                        for c in range(BODY):
                            gather(l, At(i, c, BODY))
                    for k in range(EDGE_GROUPS // BODY * BODY, EDGE_GROUPS):
                        gather(l, At(k // BODY, k % BODY, BODY))

            pool.wait_ge(s_flag, 1)
            general_needed = pool.value_load(flag[0:1, 0:1], min_val=0, max_val=1)
            with pool.If(general_needed != 0):
                general()
            with pool.Else():
                fast()

        @block.vector
        def _(dve):
            dve.wait_ge(s_in, 16 * INPUT_LOADS)
            dve.wait_ge(s_const, 7)
            dve.memset(meta[:, :, 0:1], 1.0)
            dve.tensor_copy(meta[:, :, 1], dst_tab[:, :])
            dve.tensor_copy(meta[:, :, 2], weight_tab[:, :])
            dve.tensor_copy(meta[:, :, 3], type_tab[:, :])
            dve.tensor_copy(dump_f[:, :], dump_i[:, :])
            dve.tensor_scalar(grade[:, 0, :], type_tab[:, :], float(PER_GRADE), None, ALU.is_lt)
            dve.tensor_scalar(grade[:, 2, :], type_tab[:, :], float(2 * PER_GRADE), None, ALU.is_ge)
            dve.drain()
            dve.tensor_tensor(grade[:, 1, :], grade[:, 0, :], grade[:, 2, :], ALU.add)
            dve.drain()
            dve.tensor_scalar(grade[:, 1, :], grade[:, 1, :], -1.0, 1.0, ALU.mult, ALU.add)
            dve.drain().then_inc(s_meta, 1)
            dve.wait_ge(s_const, 14)
            dve.tensor_scalar(thresh[:, :], thresh_i[:, :], float(PAD_DST), None, ALU.min)
            dve.tensor_copy(pace[:, :], pace_i[:, :])
            dve.wait_ge(s_pre, 1)
            dve.drain()
            for c in range(NG + 1):
                dve.tensor_scalar(scan[:, :], ps_rows[0][:, 0:EDGE_TILES], thresh[:, c:c + 1], 0.0, ALU.is_lt,
                                  ALU.add, accum_out=found_tile[:, c:c + 1])
                dve.drain()
            dve.tensor_copy(found_tile_i[:, :], found_tile[:, :])
            dve.drain().then_inc(s_find, 1)
            dve.wait_ge(s_found, 16 * (NG + 1))
            for c in range(NG + 1):
                dve.tensor_scalar(scan[0:NGP, 0:P], found_rows[0:NGP, c, :], thresh[0:NGP, c:c + 1], 0.0, ALU.is_lt,
                                  ALU.add, accum_out=found_in[0:NGP, c:c + 1])
                dve.drain()
            dve.memset(starts[:, :], 0.0)
            dve.drain()
            dve.scalar_tensor_tensor(out=starts[0:NGP, :], in0=found_tile[0:NGP, :], scalar=float(P),
                                     in1=found_in[0:NGP, :], op0=ALU.mult, op1=ALU.add)
            dve.drain()
            dve.memset(bad[:, :], 0.0)
            dve.tensor_tensor(bad_scr[:, :], starts[:, 1:NG + 1], starts[:, 0:NG], ALU.subtract)
            dve.drain()
            dve.tensor_scalar(bad_scr[:, :], bad_scr[:, :], float(WIN), 0.0, ALU.is_gt, ALU.add,
                              accum_out=bad[:, 0:1])
            dve.drain()
            dve.tensor_scalar(starts[:, :], starts[:, :], float(SLOTS - WIN), None, ALU.min)
            dve.drain()
            dve.tensor_scalar(bad_scr[:, :], starts[:, 0:NG], float(WIN), pace[:, 0:1], ALU.add, ALU.is_gt)
            dve.drain()
            dve.tensor_reduce(bad[:, 1:2], bad_scr[:, :], mybir.AxisListType.X, ALU.add)
            dve.wait_ge(s_order, 32)
            dve.tensor_tensor(scan[:, :], order[:, 1, :], order[:, 0, :], ALU.is_lt)
            dve.drain()
            dve.tensor_reduce(bad[:, 2:3], scan[:, :], mybir.AxisListType.X, ALU.add)
            dve.drain()
            dve.tensor_reduce(bad_sum[:, :], bad[:, :], mybir.AxisListType.X, ALU.add)
            dve.tensor_copy(starts_i[:, :], starts[:, 0:NG])
            dve.drain().then_inc(s_find, 1)
            dve.tensor_scalar(starts_hi[:, :], starts_i[:, 1:NG:2], 16, None, ALU.logical_shift_left)
            dve.drain()
            dve.tensor_tensor(starts_word[:, :], starts_i[:, 0:NG:2], starts_hi[:, :], ALU.bitwise_or)
            dve.drain().then_inc(s_find, 1)
            dve.wait_ge(s_pre, 2)
            dve.tensor_scalar(flag[:, :], ps_rows[1][0:1, 0:1], 0.5, None, ALU.is_gt).then_inc(s_flag, 1)

            def general():
                for l, before in edge_loops():
                    with dve.Fori(0, EDGE_TILES) as t:
                        dve.wait_ge(s_turn, before + 1 + t)
                        dve.wait_ge(s_dstrow, 16 * (before + 1 + t))
                        dst_col = meta[:, bass.ds(t, 1), 1]
                        dve.scalar_tensor_tensor(out=same_before[:, :], in0=dst_row[:, :], scalar=dst_col,
                                                 in1=earlier[:, :], op0=ALU.is_equal, op1=ALU.mult,
                                                 accum_out=repeats[:, :])
                        if l < LAYERS:
                            dve.tensor_scalar(same[:, :], dst_row[:, :], dst_col, meta[:, bass.ds(t, 1), 2],
                                              ALU.is_equal, ALU.mult).then_inc(s_same, 1)
                        else:
                            dve.tensor_scalar(same[:, :], dst_row[:, :], dst_col, None,
                                              ALU.is_equal).then_inc(s_same, 1)
                        dve.drain()
                        dve.tensor_scalar(repeats[:, :], repeats[:, :], 0.5, None, ALU.is_gt)
                        dve.tensor_tensor(target_f[:, :], dump_f[:, :], dst_col, ALU.subtract)
                        dve.drain()
                        dve.tensor_tensor(target_f[:, :], target_f[:, :], repeats[:, :], ALU.mult)
                        dve.drain()
                        dve.tensor_tensor(target[:, :], target_f[:, :], dst_col, ALU.add).then_inc(s_target, 1)
                        if l < LAYERS:
                            dve.tensor_copy(feats[:, D:EW], meta[:, bass.ds(t, 1), :].squeeze(1)).then_inc(s_msg, 1)
                        else:
                            dve.wait_ge(s_typed, t + 1)
                            dve.tensor_tensor(typed_msg[:, :, :].rearrange("p a b -> p (a b)"), ps_typed[:, :],
                                              typed_b[:, :, :].rearrange("p a b -> p (a b)"), ALU.add)
                            dve.drain()
                            dve.tensor_scalar(msg[:, 0:D], typed_msg[:, 0, :], grade[:, 0, bass.ds(t, 1)], None, ALU.mult)
                            for g in (1, 2):
                                dve.drain()
                                dve.scalar_tensor_tensor(out=msg[:, 0:D], in0=typed_msg[:, g, :],
                                                         scalar=grade[:, g, bass.ds(t, 1)], in1=msg[:, 0:D],
                                                         op0=ALU.mult, op1=ALU.add)
                            dve.tensor_copy(msg[:, D:EW], meta[:, bass.ds(t, 1), :].squeeze(1))
                            dve.drain().then_inc(s_msg, 1)
                    loads = NODE_TILES * sum(LOADS[:l])
                    normed = max(0, l - LAYERS + 1) * NODE_TILES
                    with dve.Fori(0, NODE_TILES) as i:
                        if l < LAYERS:
                            dve.wait_ge(s_prod, l * NODE_TILES + 1 + i)
                            dve.tensor_tensor(z2[:, :], ps_out[:, :], rel_b[:, l, :], ALU.add)
                            dve.drain()
                            if l < LAYERS - 1:
                                dve.tensor_scalar(z[:, :], z2[:, :], 0.0, None, ALU.max).then_inc(s_done, 1)
                                continue
                            dve.tensor_tensor(z2[:, :], z2[:, :], res_in[:, :], ALU.add)
                        else:
                            dve.wait_ge(s_load, 16 * loads + 16 * LOADS[l] * (i + 1))
                            dve.tensor_scalar(deg[:, :], agg_in[:, D:D + 1], 1.0, None, ALU.max)
                            dve.drain()
                            dve.reciprocal(deg[:, :], deg[:, :])
                            dve.drain()
                            dve.tensor_scalar(z2[:, :], agg_in[:, 0:D], deg[:, 0:1], 0.0, ALU.mult, ALU.max)
                            dve.drain()
                            dve.tensor_tensor(z2[:, :], z2[:, :], res_in[:, :], ALU.add)
                        dve.drain()
                        dve.bn_stats(stats[:, :], z2[:, :])
                        dve.drain()
                        dve.bn_aggr(mean_var[:, :], stats[:, :])
                        dve.drain().then_inc(s_z, 1)
                        dve.wait_ge(s_std, normed + 1 + i)
                        dve.reciprocal(rstd[:, :], std[:, :])
                        dve.drain()
                        dve.tensor_scalar(z[:, :], z2[:, :], mean_var[:, 0:1], rstd[:, 0:1], ALU.subtract,
                                          ALU.mult).then_inc(s_done, 1)

            def fast():
                def placement(l, g):
                    n = l * NGP + g.n
                    dve.wait_ge(s_win[g.slot(4)], 64 * g.uses(4, NGP, l))
                    dve.wait_ge(s_place, nth(n, 2))
                    dve.tensor_tensor(rel_dst[0:WIN, g.slot(2), :], win[0:WIN, g.slot(4), :, D + 1],
                                      tile_base[0:WIN, bass.ds(NG * g.n, NG)], ALU.subtract).then_inc(s_rel, 1)
                    dve.wait_ge(s_rel, n + 1)
                    dve.wait_ge(s_node_p, nth(n, 4))
                    for j in range(NG):
                        weighted = l < LAYERS
                        op = dve.tensor_scalar(place[0:WIN, g.slot(4), j, :], iota_row[0:WIN, :],
                                               rel_dst[0:WIN, g.slot(2), j:j + 1],
                                               win[0:WIN, g.slot(4), j, D + 2:D + 3] if weighted else None,
                                               ALU.is_equal, *([ALU.mult] if weighted else []))
                    op.then_inc(s_place, 1)

                def edges_out(l, k):
                    n = l * EDGE_GROUPS + k.n
                    dve.wait_ge(s_edge_st, 16 * nth(n, 4))
                    if l < LAYERS:
                        dve.wait_ge(s_edge_p, n + 1)
                        dve.tensor_copy(edge_out[:, k.slot(4), :, 0:D],
                                        ps_edge_out[k.slot(2)][:, :].rearrange("p (j d) -> p j d", j=NG)
                                        ).then_inc(s_edge_out, 1)
                        return
                    for j in range(NG):
                        tile = NG * k.n + j
                        dve.wait_ge(s_typed_p, tile + 1)
                        if not (isinstance(tile, int) and tile == 0):
                            dve.wait_ge(s_dve, 3 * tile)
                        dve.tensor_tensor(typed_ring[:, :], ps_edge_out[j % 2][:, 0:GRADES * D],
                                          typed_b[:, :, :].rearrange("p a b -> p (a b)"), ALU.add
                                          ).then_inc(s_typed_e, 1)
                        dve.wait_ge(s_typed_e, tile + 1)
                        msg_j = edge_out[:, k.slot(4), j, 0:D]
                        dve.tensor_scalar(msg_j, typed_ring[:, 0:D], grade[:, 0, bass.ds(tile, 1)], None,
                                          ALU.mult).then_inc(s_dve, 1)
                        for t in range(1, GRADES):
                            dve.wait_ge(s_dve, 3 * tile + t)
                            dve.scalar_tensor_tensor(out=msg_j, in0=typed_ring[:, t * D:(t + 1) * D],
                                                     scalar=grade[:, t, bass.ds(tile, 1)], in1=msg_j,
                                                     op0=ALU.mult, op1=ALU.add).then_inc(s_dve, 1)
                    dve.wait_ge(s_dve, 3 * (tile + 1))
                    dve.sem_inc(s_edge_out, 1)

                def rows_out(l, g, kept_here):
                    n = l * NGP + g.n
                    half = slice(NG * g.slot(2), NG * g.slot(2) + NG)
                    m_slot = (g.c // 2) % 2
                    if l < LAYERS - 1:
                        dve.wait_ge(s_back, nth(n))
                        free_rows(l, g)
                        dve.tensor_copy(rows[:, m_slot, half, :],
                                        ps_rows[g.slot(2)][:, :].rearrange("p (j d) -> p j d", j=NG)
                                        ).then_inc(s_rows, 1)
                        return
                    q = (l - LAYERS + 1) * NGP + g.n
                    b = g.slot(2)
                    dve.wait_ge(s_rows, nth(n, 2))
                    if l < LAYERS:
                        dve.wait_ge(s_back, nth(n))
                        dve.wait_ge(s_resid[m_slot], 16 * resid_uses(l, step_of(g)))
                        dve.tensor_tensor(pre[:, b, :, :], ps_rows[b][:, :].rearrange("p (j d) -> p j d", j=NG),
                                          resid[:, m_slot, half, :], ALU.add).then_inc(s_lnsum, 1)
                    else:
                        dve.wait_ge(s_next, nth(n))
                        if kept_here:
                            other = kept[:, bass.ds(GD * g.n, GD)].rearrange("p (j d) -> p j d", j=NG)
                        else:
                            dve.wait_ge(s_resid[m_slot], 16 * resid_uses(l, step_of(g)))
                            other = resid[:, m_slot, half, :]
                        dve.tensor_tensor(pre[:, b, :, :], next_t[:, b, :].rearrange("p (j d) -> p j d", j=NG),
                                          other, ALU.add).then_inc(s_lnsum, 1)
                    dve.wait_ge(s_lnsum, q + 1)
                    for j in range(NG):
                        op = dve.bn_stats(ln_stats[:, b, j, :], pre[:, b, j, :])
                    op.then_inc(s_ln, 1)
                    dve.wait_ge(s_ln, q + 1)
                    dve.sem_inc(s_idle, 1)
                    for j in range(NG):
                        op = dve.bn_aggr(ln_mv[:, b, j, :], ln_stats[:, b, j, :])
                    op.then_inc(s_var, 1)

                def normalise(l, g, kept_here):
                    n = l * NGP + g.n
                    q = (l - LAYERS + 1) * NGP + g.n
                    b = g.slot(2)
                    half = slice(NG * g.slot(2), NG * g.slot(2) + NG)
                    m_slot = (g.c // 2) % 2
                    dve.wait_ge(s_lnstd, q + 1)
                    dve.reciprocal(ln_rstd[:, b, :], ln_std[:, b, :]).then_inc(s_rstd, 1)
                    dve.wait_ge(s_rstd, q + 1)
                    free_rows(l, g)
                    for j in range(NG):
                        to = rows[:, m_slot, NG * g.slot(2) + j, :]
                        op = dve.tensor_scalar(to, pre[:, b, j, :], ln_mv[:, b, j, 0:1], ln_rstd[:, b, j:j + 1],
                                               ALU.subtract, ALU.mult)
                    op.then_inc(s_rows, 1)

                def degrees(g):
                    dve.wait_ge(s_node_p, nth(LAYERS * NGP + g.n))
                    dve.wait_ge(s_next, nth(LAYERS * NGP + g.n, 2))
                    dve.tensor_scalar(inv_deg[:, g.slot(2), :], ps_rows[g.slot(2)][:, 0:NG], 1.0, None, ALU.max
                                      ).then_inc(s_degmax, 1)
                    dve.wait_ge(s_degmax, g.n + 1)
                    dve.reciprocal(inv_deg[:, g.slot(2), :], inv_deg[:, g.slot(2), :]).then_inc(s_deg, 1)

                def step_of(g):
                    return At(g.i, g.c // 2, g.per // 2)

                def free_rows(l, g):
                    m = step_of(g)
                    dve.wait_ge(s_store[m.slot(2)], 16 * (CREDIT + m.uses(2, STEPS, l) - 1))

                for l in range(LAYERS + 1):
                    ln = l >= LAYERS - 1
                    if l == LAYERS:
                        dve.wait_ge(s_kept, RES_STEPS)
                    for k in range(LEAD):
                        edges_out(l, At(0, k, BODY))
                    placement(l, At(0, 0, 2 * BODY))

                    def step(m, kept_here, kept_before, first=False, last=False):
                        g = At(m.i, 2 * m.c, 2 * m.per)
                        placement(l, g.plus(1))
                        if l == LAYERS:
                            degrees(g)
                        if not first:
                            rows_out(l, g.plus(-1), kept_before)
                        if not (isinstance(m.n, int) and m.n + LEAD >= EDGE_GROUPS):
                            edges_out(l, m.plus(LEAD))
                        if ln and not first:
                            normalise(l, g.plus(-1), kept_before)
                        if not last:
                            placement(l, g.plus(2))
                        if l == LAYERS:
                            degrees(g.plus(1))
                        rows_out(l, g, kept_here)
                        if ln:
                            normalise(l, g, kept_here)

                    walk(dve, step)
                    rows_out(l, At(STEPS // BODY, 1, 2 * BODY), False)
                    if ln:
                        normalise(l, At(STEPS // BODY, 1, 2 * BODY), False)

            dve.wait_ge(s_flag, 1)
            general_needed = dve.value_load(flag[0:1, 0:1], min_val=0, max_val=1)
            with dve.If(general_needed != 0):
                general()
            with dve.Else():
                fast()

        @block.tensor
        def _(pe):
            pe.wait_ge(s_const, 7)
            pe.wait_ge(s_in, 16 * INPUT_LOADS)
            pe.wait_ge(s_meta, 1)
            pe.wait_ge(s_const, 14)
            pe.matmul(ps_rows[0][:, 0:EDGE_TILES], pick_last[:, :], meta[:, :, 1], start=True, stop=True
                      ).then_inc(s_pre, 1)
            pe.wait_ge(s_find, 2)
            pe.matmul(ps_rows[1][0:1, 0:1], bad_sum[:, :], ones_col[:, :], start=True, stop=True
                      ).then_inc(s_pre, 1)

            def general():
                for l, before in edge_loops():
                    with pe.Fori(0, EDGE_TILES) as t:
                        pe.wait_ge(s_gather, 16 * (before + 1 + t))
                        if l == LAYERS:
                            pe.transpose(ps_t[:, 0:D], feats[:, 0:D], ident[:, :]).then_inc(s_ft, 1)
                            pe.wait_ge(s_fte, t + 1)
                            pe.matmul(ps_typed[:, :], feats_t[:, :], typed_w[:, :, :].rearrange("p a b -> p (a b)"),
                                      start=True, stop=True).then_inc(s_typed, 1)
                        pe.wait_ge(s_same, before + 1 + t)
                        pe.wait_ge(s_msg, before + 1 + t)
                        pe.matmul(ps_sum[:, :], same[:, :], (msg if l == LAYERS else feats)[:, :],
                                  start=True, stop=True).then_inc(s_sum, 1)
                    if l == LAYERS:
                        continue
                    loads = NODE_TILES * sum(LOADS[:l])
                    with pe.Fori(0, NODE_TILES) as i:
                        pe.wait_ge(s_load, 16 * loads + 16 * LOADS[l] * (i + 1))
                        pe.transpose(ps_t[:, 0:D], h_in[:, :], ident[:, :])
                        pe.transpose(ps_t[:, D:2 * D], agg_in[:, 0:D], ident[:, :]).then_inc(s_tr, 1)
                        pe.wait_ge(s_tre, l * NODE_TILES + 1 + i)
                        pe.matmul(ps_out[:, :], both_t[:, 0:D], root_w[:, l, :], start=True, stop=False)
                        pe.matmul(ps_out[:, :], both_t[:, D:2 * D], rel_w[:, l, :],
                                  start=False, stop=True).then_inc(s_prod, 1)

            def fast():

                def edge_transposes(l, k):
                    n = l * EDGE_GROUPS + k.n
                    pe.wait_ge(s_gathered[k.slot(4)], 64 * k.uses(4, EDGE_GROUPS, l))
                    pe.wait_ge(s_edge_te, nth(n, 2))
                    for j in range(NG):
                        op = pe.transpose(ps_edge_t[k.slot(2)][:, j * P:(j + 1) * P],
                                          gather_ring[:, k.slot(4), j, :], ident[:, :])
                    op.then_inc(s_edge_t, 1)

                def edge_products(l, k):
                    n = l * EDGE_GROUPS + k.n
                    pe.wait_ge(s_edge_te, nth(n))
                    if l < LAYERS:
                        pe.wait_ge(s_edge_out, nth(n, 2))
                    for j in range(NG):
                        lhs = edge_t[:, k.slot(2), j * P:(j + 1) * P]
                        if l < LAYERS:
                            op = pe.matmul(ps_edge_out[k.slot(2)][:, j * D:(j + 1) * D], lhs, rel_w[:, l, :],
                                           start=True, stop=True)
                        else:
                            tile = NG * k.n + j
                            if not (isinstance(tile, int) and tile < 2):
                                pe.wait_ge(s_typed_e, tile - 1)
                            pe.matmul(ps_edge_out[j % 2][:, 0:GRADES * D], lhs,
                                      typed_w[:, :, :].rearrange("p a b -> p (a b)"),
                                      start=True, stop=True).then_inc(s_typed_p, 1)
                    if l < LAYERS:
                        op.then_inc(s_edge_p, 1)

                def nodes(l, g, kept_here):
                    n = l * NGP + g.n
                    bank = ps_node[g.slot(2)]
                    pe.wait_ge(s_next, nth(n, 2))
                    if l < LAYERS:
                        if l == 0 or not kept_here:
                            pe.wait_ge(s_feat[g.slot(4)], 16 * feat_uses(l, g))
                            feats_g = feat_t[:, g.slot(4), :]
                        else:
                            feats_g = kept[:, bass.ds(GD * g.n, GD)]
                        pe.matmul(bank[:, :], root_w[:, l, :], feats_g, start=True, stop=False)
                    pe.wait_ge(s_place, nth(n))
                    for j in range(NG):
                        w = win[0:WIN, g.slot(4), j, 0:D]
                        pl = place[0:WIN, g.slot(4), j, :]
                        if l < LAYERS:
                            op = pe.matmul(bank[:, j * P:(j + 1) * P], w, pl, start=False, stop=(j == NG - 1))
                        else:
                            pe.matmul(bank[:, j * D:(j + 1) * D], pl, w, start=True, stop=True)
                    if l == LAYERS:
                        pe.wait_ge(s_deg, nth(g.n, 2))
                        for j in range(NG):
                            op = pe.matmul(ps_rows[g.slot(2)][:, j:j + 1], place[0:WIN, g.slot(4), j, :],
                                           win[0:WIN, g.slot(4), j, D:D + 1], start=True, stop=True)
                    op.then_inc(s_node_p, 1)

                def transposes_back(l, g):
                    n = l * NGP + g.n
                    pe.wait_ge(s_next, nth(n))
                    pe.wait_ge(s_rows, nth(n, 2))
                    for j in range(NG):
                        op = pe.transpose(ps_rows[g.slot(2)][:, j * D:(j + 1) * D],
                                          next_t[:, g.slot(2), j * P:(j + 1) * P], ident[:, :])
                    op.then_inc(s_back, 1)

                for l in range(LAYERS + 1):
                    if l:
                        pe.wait_ge(s_next, nth(l * NGP - 1))
                        pe.wait_ge(s_rows, nth(l * NGP - 1))
                        pe.wait_ge(s_edge_out, nth(l * EDGE_GROUPS - 1))
                    for k in range(LEAD):
                        edge_transposes(l, At(0, k, BODY))
                        edge_products(l, At(0, k, BODY))

                    def step(m, kept_here, kept_before, first=False, last=False):
                        g = At(m.i, 2 * m.c, 2 * m.per)
                        edges = not (isinstance(m.n, int) and m.n + LEAD >= EDGE_GROUPS)
                        if edges:
                            edge_transposes(l, m.plus(LEAD))
                        nodes(l, g, kept_here)
                        if l < LAYERS and not first:
                            transposes_back(l, g.plus(-1))
                        if edges:
                            edge_products(l, m.plus(LEAD))
                        nodes(l, g.plus(1), kept_here)
                        if l < LAYERS:
                            transposes_back(l, g)

                    walk(pe, step)
                    if l < LAYERS:
                        transposes_back(l, At(STEPS // BODY, 1, 2 * BODY))

            pe.wait_ge(s_flag, 1)
            general_needed = pe.value_load(flag[0:1, 0:1], min_val=0, max_val=1)
            with pe.If(general_needed != 0):
                general()
            with pe.Else():
                fast()

        @block.scalar
        def _(act):


            def general():
                for l, before in edge_loops():
                    with act.Fori(0, EDGE_TILES) as t:
                        if l == LAYERS:
                            act.wait_ge(s_ft, t + 1)
                            act.activation(feats_t[:, :], ps_t[:, 0:D], ACT.Copy).then_inc(s_fte, 1)
                        act.wait_ge(s_sum, before + 1 + t)
                        act.activation(summed[:, :], ps_sum[:, :], ACT.Copy).then_inc(s_summed, 1)
                    with act.Fori(0, NODE_TILES) as i:
                        if l < LAYERS:
                            act.wait_ge(s_tr, l * NODE_TILES + 1 + i)
                            act.activation(both_t[:, :], ps_t[:, :], ACT.Copy).then_inc(s_tre, 1)
                        if l >= LAYERS - 1:
                            act.wait_ge(s_z, (l - LAYERS + 1) * NODE_TILES + 1 + i)
                            act.activation(std[:, :], mean_var[:, 1:2], ACT.Sqrt,
                                           bias=eps_col[:, 0:1]).then_inc(s_std, 1)

            def fast():
                act.wait_ge(s_in, 16 * INPUT_LOADS)
                act.wait_ge(s_const, 14)

                def edge_copy(l, k):
                    n = l * EDGE_GROUPS + k.n
                    act.wait_ge(s_edge_t, n + 1)
                    act.wait_ge(s_edge_out, nth(n, 2))
                    act.activation(edge_t[:, k.slot(2), :], ps_edge_t[k.slot(2)][:, :], ACT.Copy
                                   ).then_inc(s_edge_te, 1)

                def features(l, g, kept_here):
                    n = l * NGP + g.n
                    b = g.slot(2)
                    act.wait_ge(s_node_p, nth(n))
                    if l == LAYERS:
                        act.wait_ge(s_deg, nth(g.n))
                        act.wait_ge(s_rows, nth(n, 2))
                        for j in range(NG):
                            op = act.activation(next_t[:, b, j * D:(j + 1) * D], ps_node[b][:, j * D:(j + 1) * D],
                                                ACT.Relu, scale=inv_deg[:, b, j:j + 1])
                        op.then_inc(s_next, 1)
                        return
                    func = ACT.Relu if l < LAYERS - 1 else ACT.Identity
                    if l < LAYERS - 1 and kept_here:
                        act.activation(kept[:, bass.ds(GD * g.n, GD)], ps_node[b][:, :], func,
                                       bias=rel_bt[:, l:l + 1])
                    act.wait_ge(s_back, nth(n, 2))
                    act.wait_ge(s_spill[b], 16 * spills_before(l, g, kept_here))
                    act.activation(next_t[:, b, :], ps_node[b][:, :], func,
                                   bias=rel_bt[:, l:l + 1]).then_inc(s_next, 1)
                    if l < LAYERS - 1 and not kept_here:
                        act.wait_ge(s_next, nth(n))
                        act.dma_start(spill[bass.ds(g.n, 1)].squeeze(0), next_t[:, b, :]).then_inc(s_spill[b], 16)

                def deviation(l, g):
                    q = (l - LAYERS + 1) * NGP + g.n
                    act.wait_ge(s_var, q + 1)
                    act.activation(ln_std[:, g.slot(2), :], ln_mv[:, g.slot(2), :, 1], ACT.Sqrt,
                                   bias=eps_col[:, 0:1]).then_inc(s_lnstd, 1)

                def store(l, m, kept_here):
                    act.wait_ge(s_rows, nth(l * NGP + 2 * m.n + 1))
                    if l == LAYERS - 1 and kept_here:
                        act.activation(kept[:, bass.ds(2 * GD * m.n, 2 * GD)],
                                       rows[:, m.slot(2), :, :].rearrange("p j d -> p (j d)"), ACT.Copy
                                       ).then_inc(s_kept, 1)
                        act.wait_ge(s_kept, m.n + 1)
                    act.dma_start(h_steps[l + 1][bass.ds(m.n, 1)].squeeze(0), rows[:, m.slot(2), :, :]
                                  ).then_inc(s_store[m.slot(2)], 16)

                for l in range(LAYERS + 1):
                    ln = l >= LAYERS - 1
                    for k in range(LEAD):
                        edge_copy(l, At(0, k, BODY))

                    def step(m, kept_here, kept_before, first=False, last=False):
                        g = At(m.i, 2 * m.c, 2 * m.per)
                        if not (isinstance(m.n, int) and m.n + LEAD >= EDGE_GROUPS):
                            edge_copy(l, m.plus(LEAD))
                        features(l, g, kept_here)
                        if ln and not first:
                            deviation(l, g.plus(-1))
                        if not first:
                            store(l, m.plus(-1), kept_before)
                        features(l, g.plus(1), kept_here)
                        if ln:
                            deviation(l, g)

                    walk(act, step)
                    if ln:
                        deviation(l, At(STEPS // BODY, 1, 2 * BODY))
                    store(l, At(STEPS // BODY, 0, BODY), False)

            act.wait_ge(s_flag, 1)
            general_needed = act.value_load(flag[0:1, 0:1], min_val=0, max_val=1)
            with act.If(general_needed != 0):
                general()
            with act.Else():
                fast()
def kernel(**inputs):
    import numpy as _np
    import concourse.bacc as _bacc
    from concourse import mybir as _mybir
    from concourse.bass_utils import run_bass_kernel_spmd as _run

    a = {k: _np.asarray(v) for k, v in inputs.items()}

    def padded(v, rows, fill=0):
        tail = _np.full((rows - v.shape[0],) + v.shape[1:], fill, v.dtype)
        return _np.concatenate([v, tail])

    def by_tile(v, fill=0):
        return _np.ascontiguousarray(padded(v, SLOTS, fill).reshape(EDGE_TILES, P).T)

    arrays = {
        "in_x": padded(a["x"], ROWS),
        "in_x_t": _np.ascontiguousarray(padded(a["x"], ROWS).reshape(NGP, GD, D).transpose(0, 2, 1)),
        "in_src": by_tile(a["src"]),
        "in_dst": by_tile(a["dst"], PAD_DST),
        "in_dst_rows": padded(a["dst"], SLOTS + P, PAD_DST).reshape(EDGE_TILES + 1, P),
        "in_type": by_tile(a["edge_type_30"]),
        "in_weight": by_tile(a["edge_weight"]),
        "in_w_rel": a["L0_gnn_W_rel"], "in_b_rel": a["L0_gnn_b_rel"], "in_w_root": a["L0_gnn_W_root"],
        "in_w_typed": a["L1_gnn_W"], "in_b_typed": a["L1_gnn_b"],
    }
    nc = _bacc.Bacc("TRN2", target_bir_lowering=False, num_devices=1)
    args = [nc.dram_tensor(n, v.shape, _mybir.dt.from_np(v.dtype), kind="ExternalInput").ap()
            for n, v in arrays.items()]
    args.append(nc.dram_tensor("out_x", (ROWS, D), _mybir.dt.float32, kind="ExternalOutput").ap())
    gnn_kernel(nc, *args)
    r = _run(nc, [arrays], core_ids=[0])
    return r.results[0]["out_x"][:NODES]
```

```python
from contextlib import ExitStack

import concourse.bass as bass
import numpy as np
from concourse import mybir

ALU = mybir.AluOpType
ACT = mybir.ActivationFunctionType
F32 = mybir.dt.float32
I32 = mybir.dt.int32
BF16 = mybir.dt.bfloat16

P = 128
NODES = 50000
EDGES = 25000
D = 128
LAYERS = 3
GRADES = 3
PER_GRADE = 10
EPS = 1e-5
NG = 4
NODE_TILES = -(-NODES // (P * NG)) * NG
EDGE_TILES = -(-EDGES // (P * NG)) * NG
ROWS = NODE_TILES * P
SLOTS = EDGE_TILES * P
PAD_DST = ROWS - 1
META = 4
EW = D + META

STEPS = NODE_TILES // (2 * NG)
EDGE_GROUPS = EDGE_TILES // NG
BODY = 4
LEAD = 4
AHEAD = 2
HALF_BITS = 14
HALF_MASK = (1 << HALF_BITS) - 1
CUTS = NG + 3
BIAS_PARTS = 3
GD = NG * D
NGP = NODE_TILES // NG
CREDIT = 4
GATHER_LEAD = LEAD + 3
DRAIN = 2
RES_BODIES = 5
RES_STEPS = DRAIN + RES_BODIES * BODY
LOOPED = (STEPS - GATHER_LEAD) // BODY
RES_GROUPS = 2 * RES_STEPS


def nth(n, back=0):
    return n + 1 - back + CREDIT


class At:

    def __init__(self, i, c, per, looped=False):
        self.i, self.c, self.per, self.looped = i, c, per, looped
        self.n = i * per + c

    def plus(self, k):
        return At(self.i, self.c + k, self.per, self.looped)

    def slot(self, ring):
        return self.c % ring

    def outside(self, total):
        return isinstance(self.n, int) and not 0 <= self.n < total

    @property
    def kept(self):
        return self.n * BODY < RES_STEPS * self.per if isinstance(self.n, int) else self.looped

    def uses(self, ring, total, layer):
        before = layer * len(range(self.c % ring, total, ring))
        return self.i * (self.per // ring) + self.c // ring + 1 + before


def count(slot, ring, to, since=0):
    return len([n for n in range(since, to) if n % ring == slot])


class Windows:

    def __init__(self, count, nodes, edges, bits):
        self.count, self.nodes, self.edges, self.bits = count, nodes, edges, bits
        self.spans = [(j * nodes, min((j + 1) * nodes, GD)) for j in range(count)]
        self.reach = 2 * (HALF_MASK + (count - 1) * ((1 << bits) - 1)) + edges


THIRDS = Windows(3, -(-GD // 3), P, 7)
TILES = Windows(NG, P, 112, 6)
REACH = max(THIRDS.reach, TILES.reach)


def wins(l):
    return THIRDS if l < LAYERS else TILES


def win_loads(l, g):
    if l < LAYERS:
        return THIRDS.count * g.uses(4, NGP, l)
    return THIRDS.count * LAYERS * count(g.slot(4), 4, NGP) + TILES.count * g.uses(4, NGP, 0)


def stores(layers, slot):
    return layers * count(slot, 2, STEPS)


def step_of(g):
    return At(g.i, g.c // 2, g.per // 2, g.looped)


def spills(layers, slot):
    return min(layers, LAYERS - 1) * count(slot, 2, STEPS, RES_STEPS)


def spills_before(l, m):
    if l == LAYERS - 1 or m.kept:
        return 1 + spills(l, m.slot(2))
    return spills(l, m.slot(2)) + m.uses(2, STEPS, 0) - count(m.slot(2), 2, RES_STEPS)


def feat_uses(l, m):
    if l == 0:
        return m.uses(2, STEPS, 0)
    slot = m.slot(2)
    return (count(slot, 2, STEPS) + (l - 1) * count(slot, 2, STEPS, RES_STEPS)
            + m.uses(2, STEPS, 0) - count(slot, 2, RES_STEPS))


def resid_uses(l, m):
    if l < LAYERS:
        return m.uses(2, STEPS, 0)
    return count(m.slot(2), 2, STEPS) + m.uses(2, STEPS, 0) - count(m.slot(2), 2, RES_STEPS)


HALVES = (range(NG // 2), range(NG // 2, NG))


def first_halves(l):
    return HALVES if l == LAYERS else (range(NG), range(0))


def graded_before(k, j, tiles):
    return (GRADES - 1) * (NG * k.n + tiles[0]) + (j - tiles[0]) + 1


def graded_last(k, j):
    of = {0: 3 - 4 * (GRADES - 1), 1: 8 - 4 * (GRADES - 1), 2: 7 - 4 * (GRADES - 1), 3: 4}[j]
    return (GRADES - 1) * NG * k.n + of


def first_group(m):
    return At(m.i, 2 * m.c, 2 * m.per, m.looped)


def walk(engine, step):
    for m in range(DRAIN):
        step(At(0, m, BODY))
    with engine.Fori(0, RES_BODIES) as i:
        for c in range(BODY):
            step(At(i, DRAIN + c, BODY, True))
    for m in range(RES_STEPS, RES_STEPS + DRAIN):
        step(At(RES_BODIES, m - RES_BODIES * BODY, BODY))
    behind = RES_STEPS + DRAIN - (RES_BODIES + 1) * BODY
    with engine.Fori(RES_BODIES + 1, LOOPED) as i:
        for c in range(BODY):
            step(At(i, behind + c, BODY))
    for m in range(LOOPED * BODY + behind, STEPS + DRAIN):
        step(At(m // BODY, m % BODY, BODY))


def gnn_kernel(nc, x, x_t, src, dst, dst_rows, etype, weight, w_rel, b_rel, w_root, w_typed, b_typed, out):
    h_tabs = [x] + [nc.dram_tensor(f"h{l}", (ROWS, D), F32, kind="Internal").ap() for l in (1, 2, 3)] + [out]
    agg = nc.dram_tensor("agg", (ROWS + P, EW), F32, kind="Internal").ap()
    h_tiles = [h.rearrange("(t p) d -> t p d", p=P) for h in h_tabs]
    h_steps = [h.rearrange("(s t p) d -> s p t d", p=P, t=2 * NG) for h in h_tabs]
    edge_rows = nc.dram_tensor("edge_rows", (REACH, EW), F32, kind="Internal").ap()
    edge_groups = edge_rows[0:SLOTS, :].rearrange("(g t p) d -> g p t d", p=P, t=NG)
    spill = nc.dram_tensor("spill", (STEPS, D, 2 * GD), F32, kind="Internal").ap()
    starts_dram = nc.dram_tensor("starts_dram", (NGP, 2), I32, kind="Internal").ap()
    agg_tiles = agg.rearrange("(t p) d -> t p d", p=P)

    with ExitStack() as ctx:
        def sb(name, shape, dt=F32):
            return ctx.enter_context(nc.sbuf_tensor(name, shape, dt))

        def pb(name, shape):
            return ctx.enter_context(nc.psum_tensor(name, shape, F32))

        def sem(name):
            return ctx.enter_context(nc.semaphore(name))

        src_tab = sb("src_tab", [P, EDGE_TILES], I32)
        dst_tab = sb("dst_tab", [P, EDGE_TILES], I32)
        type_tab = sb("type_tab", [P, EDGE_TILES], I32)
        weight_tab = sb("weight_tab", [P, EDGE_TILES])
        meta = sb("meta", [P, EDGE_TILES, META])
        grade = sb("grade", [P, GRADES, EDGE_TILES])
        rel_w = sb("rel_w", [P, LAYERS, D])
        root_w = sb("root_w", [P, LAYERS, D])
        typed_w = sb("typed_w", [P, GRADES, D])
        rel_b = sb("rel_b", [P, LAYERS, D])
        typed_b = sb("typed_b", [P, GRADES, D])
        ident = sb("ident", [P, P])
        earlier = sb("earlier", [P, P])
        zeros = sb("zeros", [P, EW])
        eps_col = sb("eps_col", [P, 1])
        dump_i = sb("dump_i", [P, 1], I32)
        dump_f = sb("dump_f", [P, 1])

        rel_bt = sb("rel_bt", [P, LAYERS])
        iota_row = sb("iota_row", [P, THIRDS.nodes])
        third_base = sb("third_base", [P, THIRDS.count * NGP])
        tile_base = sb("tile_base", [P, NODE_TILES])
        thresh_i = sb("thresh_i", [P, CUTS], I32)
        thresh = sb("thresh", [P, CUTS])
        pick_last = sb("pick_last", [P, P])
        ones_col = sb("ones_col", [P, 1])
        found_tile = sb("found_tile", [P, CUTS])
        found_tile_i = sb("found_tile_i", [P, CUTS], I32)
        found_in = sb("found_in", [P, CUTS])
        starts = sb("starts", [P, CUTS])
        starts_i = sb("starts_i", [P, CUTS], I32)
        starts_step = sb("starts_step", [P, 1], I32)
        starts_word = sb("starts_word", [P, 2], I32)
        bias_part = sb("bias_part", [P, GRADES * D], BF16)
        bias_parts = sb("bias_parts", [P, GRADES * D], BF16)
        bias_ones = sb("bias_ones", [P, P], BF16)
        pace_i = sb("pace_i", [P, 1], I32)
        pace = sb("pace", [P, 1])
        bad = sb("bad", [P, 4])
        bad_scr = sb("bad_scr", [P, CUTS])
        bad_sum = sb("bad_sum", [P, 1])
        flag = sb("flag", [1, 1], I32)
        words = sb("words", [1, 2 * NGP], I32)
        kept = sb("kept", [P, RES_GROUPS * GD])
        src_ring = sb("src_ring", [P, 4, NG], I32)
        gather_ring = sb("gather_ring", [P, 4, NG, D])
        edge_t = sb("edge_t", [P, 2, GD])
        edge_out = sb("edge_out", [P, 4, NG, EW])
        typed_ring = sb("typed_ring", [P, GRADES * D])
        win = sb("win", [P, 4, NG, EW])
        feat_t = sb("feat_t", [P, 2, 2 * GD])
        rel_dst = sb("rel_dst", [P, 2, NG])
        place = sb("place", [P, 4, GD])
        next_t = sb("next_t", [P, 4, GD])
        rows = sb("rows", [P, 2, 2 * NG, D])
        resid = sb("resid", [P, 2, 2 * NG, D])
        pre = sb("pre", [P, 4, NG, D])
        ln_stats = sb("ln_stats", [P, 4, NG, 6])
        ln_mv = sb("ln_mv", [P, 4, NG, 2])
        ln_std = sb("ln_std", [P, 4, NG])
        ln_rstd = sb("ln_rstd", [P, 4, NG])
        ln_shift = sb("ln_shift", [P, 4, NG])
        inv_deg = sb("inv_deg", [P, 2, NG])
        carved = [0]

        def carve(shape, dt=F32):
            width = int(np.prod(shape[1:]))
            view = kept[:, carved[0]:carved[0] + width]
            carved[0] += width
            if dt is not F32:
                view = view.bitcast(dt)
            return view if len(shape) == 2 else view.rearrange("p (a b) -> p a b", b=shape[2])

        scan = carve([P, EDGE_TILES])
        found_rows = carve([P, CUTS, P], I32)
        order = carve([P, 2, EDGE_TILES], I32)
        src_slot = carve([P, 1], I32)
        dst_row = carve([P, P], I32)
        feats = carve([P, EW])
        same = carve([P, P])
        same_before = carve([P, P])
        repeats = carve([P, 1])
        target_f = carve([P, 1])
        target = carve([P, 1], I32)
        feats_t = carve([P, D])
        typed_msg = carve([P, GRADES, D])
        msg = carve([P, EW])
        summed = carve([P, EW])
        h_in = carve([P, D])
        agg_in = carve([P, EW])
        res_in = carve([P, D])
        both_t = carve([P, 2 * D])
        z = carve([P, D])
        z2 = carve([P, D])
        stats = carve([P, 6])
        mean_var = carve([P, 2])
        std = carve([P, 1])
        rstd = carve([P, 1])
        deg = carve([P, 1])
        ps_edge_t = [pb(f"ps_edge_t{b}", [P, GD]) for b in range(2)]
        ps_edge_out = [pb(f"ps_edge_out{b}", [P, GD]) for b in range(2)]
        ps_node = [pb(f"ps_node{b}", [P, GD]) for b in range(2)]
        ps_rows = [pb(f"ps_rows{b}", [P, GD]) for b in range(2)]

        def typed_bank(j):
            return (ps_edge_out[0], ps_edge_out[1], ps_edge_t[1], ps_edge_out[1])[j]

        ps_t = ps_edge_t[0][:, 0:2 * D]
        ps_typed = ps_edge_out[0][:, 0:GRADES * D]
        ps_sum = ps_node[0][:, 0:EW]
        ps_out = ps_rows[0][:, 0:D]

        s_in = sem("s_in")
        s_const = sem("s_const")
        s_meta = sem("s_meta")
        s_zeroed = sem("s_zeroed")
        s_scatter = sem("s_scatter")
        s_turn = sem("s_turn")
        s_slot = sem("s_slot")
        s_gather = sem("s_gather")
        s_dstrow = sem("s_dstrow")
        s_same = sem("s_same")
        s_target = sem("s_target")
        s_ft = sem("s_ft")
        s_fte = sem("s_fte")
        s_typed = sem("s_typed")
        s_msg = sem("s_msg")
        s_sum = sem("s_sum")
        s_summed = sem("s_summed")
        s_node = sem("s_node")
        s_load = sem("s_load")
        s_tr = sem("s_tr")
        s_tre = sem("s_tre")
        s_prod = sem("s_prod")
        s_z = sem("s_z")
        s_std = sem("s_std")
        s_done = sem("s_done")
        s_nop = sem("s_nop")

        s_flag = sem("s_flag")
        s_pre = sem("s_pre")
        s_find = sem("s_find")
        s_found = sem("s_found")
        s_words = sem("s_words")
        s_order = sem("s_order")
        s_src = sem("s_src")
        s_gathered = [sem(f"s_gathered{b}") for b in range(4)]
        s_edge_t = sem("s_edge_t")
        s_edge_te = sem("s_edge_te")
        s_edge_p = sem("s_edge_p")
        s_typed_p = sem("s_typed_p")
        s_first = sem("s_first")
        s_graded = sem("s_graded")
        s_bias = sem("s_bias")
        s_shift = sem("s_shift")
        s_edge_out = sem("s_edge_out")
        s_edge_meta = sem("s_edge_meta")
        s_edge_st = [sem(f"s_edge_st{b}") for b in range(4)]
        s_win = [sem(f"s_win{b}") for b in range(4)]
        s_feat = [sem(f"s_feat{b}") for b in range(2)]
        s_resid = [sem(f"s_resid{b}") for b in range(2)]
        s_rel = sem("s_rel")
        s_place = sem("s_place")
        s_node_p = sem("s_node_p")
        s_next = sem("s_next")
        s_spill = [sem(f"s_spill{b}") for b in range(2)]
        s_back = sem("s_back")
        s_rows = sem("s_rows")
        s_store = [sem(f"s_store{b}") for b in range(2)]
        s_var = sem("s_var")
        s_lnstd = sem("s_lnstd")
        s_deg = sem("s_deg")
        s_degmax = sem("s_degmax")
        s_lnsum = sem("s_lnsum")
        s_ln = sem("s_ln")
        s_rstd = sem("s_rstd")
        s_idle = sem("s_idle")

        INPUT_LOADS = 10
        block = ctx.enter_context(nc.Block())

        def edge_loops():
            return [(l, l * EDGE_TILES) for l in range(LAYERS + 1)]

        LOADS = [2, 2, 3, 2]

        @block.sync
        def _(sp):
            for to, of in ((src_tab, src), (dst_tab, dst), (type_tab, etype), (weight_tab, weight)):
                sp.dma_start(to[:, :], of).then_inc(s_in, 16)
            sp.dma_start(rel_w[:, :, :], w_rel.rearrange("l k n -> k l n")).then_inc(s_in, 16)
            sp.dma_start(root_w[:, :, :], w_root.rearrange("l k n -> k l n")).then_inc(s_in, 16)
            sp.dma_start(typed_w[:, :, :], w_typed.rearrange("l k n -> k l n")).then_inc(s_in, 16)
            sp.dma_start(rel_b[:, :, :], b_rel.partition_broadcast(P)).then_inc(s_in, 16)
            sp.dma_start(typed_b[:, :, :], b_typed.partition_broadcast(P)).then_inc(s_in, 16)
            sp.dma_start(rel_bt[:, :], b_rel.rearrange("l d -> d l"), allow_slow_non_contiguous=True
                         ).then_inc(s_in, 16)
            flat = dst_rows.rearrange("t p -> (t p)")
            sp.dma_start(order[:, 0, :], flat[0:SLOTS].rearrange("(p t) -> p t", p=P)).then_inc(s_order, 16)
            sp.dma_start(order[:, 1, :], flat[1:SLOTS + 1].rearrange("(p t) -> p t", p=P)).then_inc(s_order, 16)
            sp.wait_ge(s_find, 3)
            sp.dma_start(starts_dram[:, :], starts_word[0:NGP, :]).then_inc(s_words, 16)
            sp.wait_ge(s_words, 16)
            sp.dma_start(words[:, :], starts_dram.rearrange("(o g) w -> o (g w)", o=1)).then_inc(s_words, 16)
            sp.wait_ge(s_words, 32)

            def general():
                sp.wait_ge(s_const, 1)
                sp.dma_start(agg_tiles.rearrange("t p d -> p t d"),
                             zeros[:, :].unsqueeze(1).broadcast_to([P, NODE_TILES + 1, EW])).then_inc(s_zeroed, 16)
                loads = 0
                for l, before in edge_loops():
                    with sp.Fori(0, EDGE_TILES) as t:
                        sp.wait_ge(s_turn, before + 1 + t)
                        sp.dma_start(dst_row[:, :], dst_rows[bass.ds(t, 1), :].squeeze(0).partition_broadcast(P)
                                     ).then_inc(s_dstrow, 16)
                    sp.wait_ge(s_turn, before + EDGE_TILES + 1)
                    with sp.Fori(0, NODE_TILES) as i:
                        sp.wait_ge(s_node, 32 * (l * NODE_TILES + 1 + i))
                        sp.dma_start(agg_in[:, :], agg_tiles[bass.ds(i, 1)].squeeze(0)).then_inc(s_load, 16)
                        if l < LAYERS:
                            sp.dma_start(h_in[:, :], h_tiles[l][bass.ds(i, 1)].squeeze(0)).then_inc(s_load, 16)
                        if l >= LAYERS - 1:
                            res = x.rearrange("(t p) d -> t p d", p=P) if l == LAYERS - 1 else h_tiles[LAYERS]
                            sp.dma_start(res_in[:, :], res[bass.ds(i, 1)].squeeze(0)).then_inc(s_load, 16)
                        sp.wait_ge(s_load, 16 * loads + 16 * LOADS[l] * (i + 1))
                        sp.dma_start(agg_tiles[bass.ds(i, 1)].squeeze(0), zeros[:, :]).then_inc(s_node, 16)
                        sp.wait_ge(s_done, l * NODE_TILES + 1 + i)
                        sp.dma_start(h_tiles[l + 1][bass.ds(i, 1)].squeeze(0), z[:, :]).then_inc(s_node, 16)
                    loads += LOADS[l] * NODE_TILES
                sp.wait_ge(s_node, 32 * (NODE_TILES * (LAYERS + 1) + 1))

            def fast():
                def load_windows(l, g):
                    sp.wait_ge(s_node_p, nth(l * NGP + g.n, 4))
                    word = sp.value_load(words[0:1, bass.ds(2 * g.n + l // LAYERS, 1)])
                    half = word & HALF_MASK
                    kind = wins(l)
                    for j in range(kind.count):
                        if j:
                            shift = HALF_BITS + kind.bits * (j - 1)
                            half = sp.snap(half + ((word >> shift) & ((1 << kind.bits) - 1)))
                        sp.dma_start(win[0:kind.edges, g.slot(4), j, :],
                                     edge_rows[bass.ds(2 * half, kind.edges), :]).then_inc(s_win[g.slot(4)], 16)

                def load_step(l, m):
                    if m.outside(STEPS):
                        return
                    for k in ([m] if isinstance(m.n, int) and m.n == 0 else []) + [m.plus(1)]:
                        if not k.outside(EDGE_GROUPS):
                            sp.wait_ge(s_edge_st[k.slot(4)], 16 * (k.uses(4, EDGE_GROUPS, l) + 1))
                            sp.sem_inc(s_idle, 1)
                    load_windows(l, first_group(m))
                    load_windows(l, first_group(m).plus(1))

                for l in range(LAYERS + 1):
                    if l:
                        for b in range(2):
                            sp.wait_ge(s_store[b], 16 * (1 + stores(l, b)))
                            sp.wait_ge(s_spill[b], 16 * (1 + spills(l, b)))

                    walk(sp, lambda m: load_step(l, m))
                for b in range(2):
                    sp.wait_ge(s_store[b], 16 * (1 + stores(LAYERS + 1, b)))

            sp.wait_ge(s_flag, 1)
            general_needed = sp.value_load(flag[0:1, 0:1], min_val=0, max_val=1)
            with sp.If(general_needed != 0):
                general()
            with sp.Else():
                fast()

        @block.gpsimd
        def _(pool):
            pool.memset(zeros[:, :], 0.0).then_inc(s_const, 1)
            pool.memset(ident[:, :], 0.0).then_inc(s_const, 1)
            pool.memset(earlier[:, :], 1.0).then_inc(s_const, 1)
            pool.memset(eps_col[:, :], EPS).then_inc(s_const, 1)
            pool.wait_ge(s_const, 4)
            pool.affine_select(out=ident[:, :], in_=ident[:, :], compare_op=ALU.not_equal, fill=1.0, base=0,
                               pattern=[[-1, P]], channel_multiplier=1).then_inc(s_const, 1)
            pool.affine_select(out=earlier[:, :], in_=earlier[:, :], compare_op=ALU.is_gt, fill=0.0, base=0,
                               pattern=[[-1, P]], channel_multiplier=1).then_inc(s_const, 1)
            pool.iota(dump_i[:, :], pattern=[[0, 1]], base=ROWS, channel_multiplier=1).then_inc(s_const, 1)

            pool.iota(iota_row[:, :], pattern=[[1, THIRDS.nodes]], base=0, channel_multiplier=0,
                      allow_small_or_imprecise_dtypes=True).then_inc(s_const, 1)
            for kind, to in ((THIRDS, third_base), (TILES, tile_base)):
                pool.iota(to[:, :], pattern=[[GD, NGP], [kind.nodes, kind.count]], base=0, channel_multiplier=0,
                          allow_small_or_imprecise_dtypes=True).then_inc(s_const, 1)
            pool.iota(thresh_i[:, 0:NG + 1], pattern=[[P, NG + 1]], base=0, channel_multiplier=GD).then_inc(s_const, 1)
            pool.iota(thresh_i[:, NG + 1:], pattern=[[THIRDS.nodes, 2]], base=THIRDS.nodes, channel_multiplier=GD
                      ).then_inc(s_const, 1)
            pool.iota(pace_i[:, :], pattern=[[0, 1]], base=AHEAD * GD - GD // 2,
                      channel_multiplier=GD // 2).then_inc(s_const, 1)
            pool.memset(pick_last[:, :], 1.0).then_inc(s_const, 1)
            pool.memset(ones_col[:, :], 1.0).then_inc(s_const, 1)
            pool.wait_ge(s_const, 15)
            pool.affine_select(out=pick_last[:, :], in_=pick_last[:, :], compare_op=ALU.is_ge, fill=0.0,
                               base=1 - P, pattern=[[0, P]], channel_multiplier=1).then_inc(s_const, 1)
            for ring in (s_edge_te, s_edge_out, s_edge_meta, s_node_p, s_next, s_back, s_rows, s_place, s_deg, s_lnsum):
                pool.sem_inc(ring, CREDIT)
            for ring in (*s_edge_st, *s_store, *s_spill):
                pool.sem_inc(ring, 16)
            pool.wait_ge(s_in, 16 * INPUT_LOADS)
            pool.wait_ge(s_meta, 1)
            pool.wait_ge(s_find, 1)
            for c in range(CUTS):
                pool.indirect_dma_start(out=found_rows[0:NGP, c, :], out_offset=None, in_=dst_rows[:, :],
                                        in_offset=bass.IndirectOffsetOnAxis(ap=found_tile_i[0:NGP, c:c + 1], axis=0)
                                        ).then_inc(s_found, 16)

            def indices(l, k):
                if k.outside(EDGE_GROUPS):
                    return
                pool.wait_ge(s_edge_te, nth(l * EDGE_GROUPS + k.n, 4))
                pool.tensor_copy(src_ring[:, k.slot(4), :], src_tab[:, bass.ds(NG * k.n, NG)]).then_inc(s_src, 1)

            def gather(l, k, tiles):
                if k.outside(EDGE_GROUPS):
                    return
                pool.wait_ge(s_src, l * EDGE_GROUPS + k.n + 1)
                pool.sem_inc(s_idle, 1)
                for j in tiles:
                    pool.indirect_dma_start(
                        out=gather_ring[:, k.slot(4), j, :], out_offset=None, in_=h_tabs[l][:, :],
                        in_offset=bass.IndirectOffsetOnAxis(ap=src_ring[:, k.slot(4), j:j + 1], axis=0)
                    ).then_inc(s_gathered[k.slot(4)], 16)

            def columns(l, k):
                if k.outside(EDGE_GROUPS):
                    return
                pool.wait_ge(s_edge_st[k.slot(4)], 16 * k.uses(4, EDGE_GROUPS, l))
                pool.tensor_copy(edge_out[:, k.slot(4), :, D:EW], meta[:, bass.ds(NG * k.n, NG), :]
                                 ).then_inc(s_edge_meta, 1)

            for k in range(BODY):
                indices(0, At(0, k, BODY))
                gather(0, At(0, k, BODY), range(NG))

            def general():
                for ring in s_gathered:
                    pool.wait_ge(ring, 16 * NG)
                pool.sem_inc(s_node, 32)
                pool.wait_ge(s_zeroed, 16)
                pool.sem_inc(s_turn, 1)
                for l, before in edge_loops():
                    if l:
                        pool.wait_ge(s_node, 32 * (l * NODE_TILES + 1))
                    with pool.Fori(0, EDGE_TILES) as t:
                        pool.wait_ge(s_turn, before + 1 + t)
                        pool.tensor_copy(src_slot[:, :], src_tab[:, bass.ds(t, 1)]).then_inc(s_slot, 1)
                        pool.wait_ge(s_slot, before + 1 + t)
                        pool.sem_inc(s_nop, 1)
                        pool.indirect_dma_start(out=feats[:, 0:D], out_offset=None, in_=h_tabs[l][:, :],
                                                in_offset=bass.IndirectOffsetOnAxis(ap=src_slot[:, 0:1], axis=0)
                                                ).then_inc(s_gather, 16)
                        pool.wait_ge(s_target, before + 1 + t)
                        pool.wait_ge(s_summed, before + 1 + t)
                        pool.sem_inc(s_nop, 1)
                        pool.indirect_dma_start(out=agg[:, :], in_=summed[:, :], in_offset=None,
                                                out_offset=bass.IndirectOffsetOnAxis(ap=target[:, 0:1], axis=0),
                                                compute_op=ALU.add).then_inc(s_scatter, 16)
                        pool.wait_ge(s_scatter, 16 * (before + 1 + t))
                        pool.sem_inc(s_turn, 1)

            def fast():
                def gather_group(l, k):
                    indices(l, k)
                    gather(l, k, range(NG))
                    columns(l, k)

                def add_residual(g):
                    if g.outside(NGP):
                        return
                    n = LAYERS * NGP + g.n
                    half = slice(NG * g.slot(2), NG * g.slot(2) + NG)
                    m = step_of(g)
                    pool.wait_ge(s_rows, nth(n, 4))
                    if g.kept:
                        other = kept[:, bass.ds(GD * g.n, GD)].rearrange("p (j d) -> p j d", j=NG)
                    else:
                        pool.wait_ge(s_resid[m.slot(2)], 16 * resid_uses(LAYERS, m))
                        other = resid[:, m.slot(2), half, :]
                    pool.wait_ge(s_next, nth(n))
                    pool.sem_inc(s_idle, 1)
                    pool.tensor_tensor(pre[:, g.slot(4), :, :],
                                       next_t[:, g.slot(4), :].rearrange("p (j d) -> p j d", j=NG),
                                       other, ALU.add).then_inc(s_lnsum, 1)

                for l in range(LAYERS + 1):
                    if l:
                        for b in range(2):
                            pool.wait_ge(s_store[b], 16 * (1 + stores(l, b)))
                    if l < LAYERS:
                        if l == 0:
                            for k in range(BODY):
                                columns(l, At(0, k, BODY))
                        with pool.Fori(0 if l else 1, EDGE_GROUPS // BODY) as i:
                            for c in range(BODY):
                                gather_group(l, At(i, c, BODY))
                        for k in range(EDGE_GROUPS // BODY * BODY, EDGE_GROUPS):
                            gather_group(l, At(k // BODY, k % BODY, BODY))
                        continue
                    for k in range(GATHER_LEAD):
                        gather_group(l, At(0, k, BODY))

                    def step(m):
                        k = m.plus(GATHER_LEAD)
                        indices(l, k)
                        for b, tiles in enumerate(HALVES):
                            add_residual(first_group(m).plus(b - 2))
                            gather(l, k, tiles)
                        columns(l, k)

                    walk(pool, step)

            pool.wait_ge(s_flag, 1)
            general_needed = pool.value_load(flag[0:1, 0:1], min_val=0, max_val=1)
            with pool.If(general_needed != 0):
                general()
            with pool.Else():
                fast()

        @block.vector
        def _(dve):
            dve.wait_ge(s_in, 16 * INPUT_LOADS)
            dve.wait_ge(s_const, 7)
            dve.memset(meta[:, :, 0:1], 1.0)
            dve.tensor_copy(meta[:, :, 1], dst_tab[:, :])
            dve.tensor_copy(meta[:, :, 2], weight_tab[:, :])
            dve.tensor_copy(meta[:, :, 3], type_tab[:, :])
            dve.tensor_copy(dump_f[:, :], dump_i[:, :])
            dve.tensor_scalar(grade[:, 0, :], type_tab[:, :], float(PER_GRADE), None, ALU.is_lt)
            dve.tensor_scalar(grade[:, 2, :], type_tab[:, :], float(2 * PER_GRADE), None, ALU.is_ge)
            dve.drain()
            dve.tensor_tensor(grade[:, 1, :], grade[:, 0, :], grade[:, 2, :], ALU.add)
            dve.drain()
            dve.tensor_scalar(grade[:, 1, :], grade[:, 1, :], -1.0, 1.0, ALU.mult, ALU.add)
            dve.drain().then_inc(s_meta, 1)
            dve.wait_ge(s_const, 16)
            dve.tensor_scalar(thresh[:, :], thresh_i[:, :], float(PAD_DST), None, ALU.min)
            dve.tensor_copy(pace[:, :], pace_i[:, :])
            dve.wait_ge(s_pre, 1)
            dve.drain()
            for c in range(CUTS):
                dve.tensor_scalar(scan[:, :], ps_rows[0][:, 0:EDGE_TILES], thresh[:, c:c + 1], 0.0, ALU.is_lt,
                                  ALU.add, accum_out=found_tile[:, c:c + 1])
                dve.drain()
            dve.tensor_copy(found_tile_i[:, :], found_tile[:, :])
            dve.drain().then_inc(s_find, 1)
            dve.wait_ge(s_found, 16 * CUTS)
            for c in range(CUTS):
                dve.tensor_scalar(scan[0:NGP, 0:P], found_rows[0:NGP, c, :], thresh[0:NGP, c:c + 1], 0.0, ALU.is_lt,
                                  ALU.add, accum_out=found_in[0:NGP, c:c + 1])
                dve.drain()
            dve.memset(starts[:, :], 0.0)
            dve.drain()
            dve.scalar_tensor_tensor(out=starts[0:NGP, :], in0=found_tile[0:NGP, :], scalar=float(P),
                                     in1=found_in[0:NGP, :], op0=ALU.mult, op1=ALU.add)
            dve.drain()
            dve.memset(bad[:, :], 0.0)
            dve.memset(bad_scr[:, :], 0.0)
            dve.drain()
            dve.tensor_tensor(bad_scr[:, 0:NG], starts[:, 1:NG + 1], starts[:, 0:NG], ALU.subtract)
            dve.drain()
            dve.tensor_scalar(bad_scr[:, 0:NG], bad_scr[:, 0:NG], float(TILES.edges - 1), 0.0, ALU.is_gt, ALU.add,
                              accum_out=bad[:, 0:1])
            dve.drain()
            for j, (a, b) in enumerate(((0, NG + 1), (NG + 1, NG + 2), (NG + 2, NG))):
                dve.tensor_tensor(bad_scr[:, j:j + 1], starts[:, b:b + 1], starts[:, a:a + 1], ALU.subtract)
            dve.drain()
            dve.tensor_scalar(bad_scr[:, 0:3], bad_scr[:, 0:3], float(THIRDS.edges - 1), 0.0, ALU.is_gt, ALU.add,
                              accum_out=bad[:, 1:2])
            dve.drain()
            dve.tensor_scalar(starts[:, :], starts[:, :], float(SLOTS - P), None, ALU.min)
            dve.drain()
            for a, b in ((0, NG), (NG + 1, CUTS)):
                dve.tensor_scalar(bad_scr[:, a:b], starts[:, a:b], float(P), pace[:, 0:1], ALU.add, ALU.is_gt)
            dve.memset(bad_scr[:, NG:NG + 1], 0.0)
            dve.drain()
            dve.tensor_reduce(bad[:, 2:3], bad_scr[:, :], mybir.AxisListType.X, ALU.add)
            dve.wait_ge(s_order, 32)
            dve.tensor_tensor(scan[:, :], order[:, 1, :], order[:, 0, :], ALU.is_lt)
            dve.drain()
            dve.tensor_reduce(bad[:, 3:4], scan[:, :], mybir.AxisListType.X, ALU.add)
            dve.drain()
            dve.tensor_reduce(bad_sum[:, :], bad[:, :], mybir.AxisListType.X, ALU.add)
            dve.drain().then_inc(s_find, 1)
            dve.wait_ge(s_pre, 2)
            dve.tensor_scalar(flag[:, :], ps_rows[1][0:1, 0:1], 0.5, None, ALU.is_gt).then_inc(s_flag, 1)
            dve.tensor_copy(starts_i[:, :], starts[:, :])
            dve.drain()
            dve.tensor_scalar(starts_i[:, :], starts_i[:, :], 1, None, ALU.logical_shift_right)
            dve.drain()
            for w, (kind, cols) in enumerate(((THIRDS, (0, NG + 1, NG + 2)), (TILES, range(NG)))):
                word = starts_word[:, w:w + 1]
                dve.tensor_copy(word, starts_i[:, 0:1])
                for j, (a, b) in enumerate(zip(cols, cols[1:])):
                    dve.tensor_tensor(starts_step[:, :], starts_i[:, b:b + 1], starts_i[:, a:a + 1], ALU.subtract)
                    dve.drain()
                    dve.tensor_scalar(starts_step[:, :], starts_step[:, :], HALF_BITS + kind.bits * j, None,
                                      ALU.logical_shift_left)
                    dve.drain()
                    dve.tensor_tensor(word, word, starts_step[:, :], ALU.bitwise_or)
                    dve.drain()
            dve.drain().then_inc(s_find, 1)
            bias_row = typed_b[:, :, :].rearrange("p a b -> p (a b)")
            dve.tensor_copy(bias_part[:, :], bias_row)
            dve.drain()
            dve.tensor_tensor(typed_ring[:, :], bias_row, bias_part[:, :], ALU.subtract)
            dve.tensor_scalar(bias_parts[:, :], bias_part[:, :], ident[:, 0:1], None, ALU.mult)
            dve.drain()
            for part in range(1, BIAS_PARTS):
                dve.tensor_copy(bias_part[:, :], typed_ring[:, :])
                dve.drain()
                dve.tensor_tensor(typed_ring[:, :], typed_ring[:, :], bias_part[:, :], ALU.subtract)
                dve.scalar_tensor_tensor(out=bias_parts[:, :], in0=bias_part[:, :], scalar=ident[:, part:part + 1],
                                         in1=bias_parts[:, :], op0=ALU.mult, op1=ALU.add)
                dve.drain()
            dve.memset(bias_ones[:, :], 1.0)
            dve.drain().then_inc(s_bias, 1)
            def general():
                for l, before in edge_loops():
                    with dve.Fori(0, EDGE_TILES) as t:
                        dve.wait_ge(s_turn, before + 1 + t)
                        dve.wait_ge(s_dstrow, 16 * (before + 1 + t))
                        dst_col = meta[:, bass.ds(t, 1), 1]
                        dve.scalar_tensor_tensor(out=same_before[:, :], in0=dst_row[:, :], scalar=dst_col,
                                                 in1=earlier[:, :], op0=ALU.is_equal, op1=ALU.mult,
                                                 accum_out=repeats[:, :])
                        if l < LAYERS:
                            dve.tensor_scalar(same[:, :], dst_row[:, :], dst_col, meta[:, bass.ds(t, 1), 2],
                                              ALU.is_equal, ALU.mult).then_inc(s_same, 1)
                        else:
                            dve.tensor_scalar(same[:, :], dst_row[:, :], dst_col, None,
                                              ALU.is_equal).then_inc(s_same, 1)
                        dve.drain()
                        dve.tensor_scalar(repeats[:, :], repeats[:, :], 0.5, None, ALU.is_gt)
                        dve.tensor_tensor(target_f[:, :], dump_f[:, :], dst_col, ALU.subtract)
                        dve.drain()
                        dve.tensor_tensor(target_f[:, :], target_f[:, :], repeats[:, :], ALU.mult)
                        dve.drain()
                        dve.tensor_tensor(target[:, :], target_f[:, :], dst_col, ALU.add).then_inc(s_target, 1)
                        if l < LAYERS:
                            dve.tensor_copy(feats[:, D:EW], meta[:, bass.ds(t, 1), :].squeeze(1)).then_inc(s_msg, 1)
                        else:
                            dve.wait_ge(s_typed, t + 1)
                            dve.tensor_tensor(typed_msg[:, :, :].rearrange("p a b -> p (a b)"), ps_typed[:, :],
                                              typed_b[:, :, :].rearrange("p a b -> p (a b)"), ALU.add)
                            dve.drain()
                            dve.tensor_scalar(msg[:, 0:D], typed_msg[:, 0, :], grade[:, 0, bass.ds(t, 1)], None, ALU.mult)
                            for g in (1, 2):
                                dve.drain()
                                dve.scalar_tensor_tensor(out=msg[:, 0:D], in0=typed_msg[:, g, :],
                                                         scalar=grade[:, g, bass.ds(t, 1)], in1=msg[:, 0:D],
                                                         op0=ALU.mult, op1=ALU.add)
                            dve.tensor_copy(msg[:, D:EW], meta[:, bass.ds(t, 1), :].squeeze(1))
                            dve.drain().then_inc(s_msg, 1)
                    loads = NODE_TILES * sum(LOADS[:l])
                    normed = max(0, l - LAYERS + 1) * NODE_TILES
                    with dve.Fori(0, NODE_TILES) as i:
                        if l < LAYERS:
                            dve.wait_ge(s_prod, l * NODE_TILES + 1 + i)
                            dve.tensor_tensor(z2[:, :], ps_out[:, :], rel_b[:, l, :], ALU.add)
                            dve.drain()
                            if l < LAYERS - 1:
                                dve.tensor_scalar(z[:, :], z2[:, :], 0.0, None, ALU.max).then_inc(s_done, 1)
                                continue
                            dve.tensor_tensor(z2[:, :], z2[:, :], res_in[:, :], ALU.add)
                        else:
                            dve.wait_ge(s_load, 16 * loads + 16 * LOADS[l] * (i + 1))
                            dve.tensor_scalar(deg[:, :], agg_in[:, D:D + 1], 1.0, None, ALU.max)
                            dve.drain()
                            dve.reciprocal(deg[:, :], deg[:, :])
                            dve.drain()
                            dve.tensor_scalar(z2[:, :], agg_in[:, 0:D], deg[:, 0:1], 0.0, ALU.mult, ALU.max)
                            dve.drain()
                            dve.tensor_tensor(z2[:, :], z2[:, :], res_in[:, :], ALU.add)
                        dve.drain()
                        dve.bn_stats(stats[:, :], z2[:, :])
                        dve.drain()
                        dve.bn_aggr(mean_var[:, :], stats[:, :])
                        dve.drain().then_inc(s_z, 1)
                        dve.wait_ge(s_std, normed + 1 + i)
                        dve.reciprocal(rstd[:, :], std[:, :])
                        dve.drain()
                        dve.tensor_scalar(z[:, :], z2[:, :], mean_var[:, 0:1], rstd[:, 0:1], ALU.subtract,
                                          ALU.mult).then_inc(s_done, 1)

            def fast():
                def window_nodes(l, g):
                    if g.outside(NGP):
                        return
                    n = l * NGP + g.n
                    kind = wins(l)
                    at = g.slot(4)
                    base = third_base if kind is THIRDS else tile_base
                    dve.wait_ge(s_win[at], 16 * win_loads(l, g))
                    dve.wait_ge(s_place, nth(n, 2))
                    dve.tensor_tensor(rel_dst[0:kind.edges, g.slot(2), 0:kind.count],
                                      win[0:kind.edges, at, 0:kind.count, D + 1],
                                      base[0:kind.edges, bass.ds(kind.count * g.n, kind.count)], ALU.subtract
                                      ).then_inc(s_rel, 1)

                def placement(l, g):
                    if g.outside(NGP):
                        return
                    n = l * NGP + g.n
                    kind = wins(l)
                    at = g.slot(4)
                    weighted = l < LAYERS
                    dve.wait_ge(s_rel, n + 1)
                    dve.wait_ge(s_node_p, nth(n, 4))
                    for j, (lo, hi) in enumerate(kind.spans):
                        op = dve.tensor_scalar(place[0:kind.edges, at, lo:hi], iota_row[0:kind.edges, 0:hi - lo],
                                               rel_dst[0:kind.edges, g.slot(2), j:j + 1],
                                               win[0:kind.edges, at, j, D + 2:D + 3] if weighted else None,
                                               ALU.is_equal, *([ALU.mult] if weighted else []))
                    op.then_inc(s_place, 1)

                def first_edges_out(l, k):
                    if k.outside(EDGE_GROUPS):
                        return
                    dve.wait_ge(s_edge_st[k.slot(4)], 16 * k.uses(4, EDGE_GROUPS, l))
                    dve.wait_ge(s_edge_p, l * EDGE_GROUPS + k.n + 1)
                    dve.tensor_copy(edge_out[:, k.slot(4), :, 0:D],
                                    ps_edge_out[k.slot(2)][:, :].rearrange("p (j d) -> p j d", j=NG)
                                    ).then_inc(s_edge_out, 1)

                def grade_edges(k, t, tiles):
                    if k.outside(EDGE_GROUPS):
                        return
                    for j in tiles:
                        tile = NG * k.n + j
                        if t == 1:
                            dve.wait_ge(s_first, tile + 1)
                        else:
                            dve.wait_ge(s_graded, graded_before(k, j, tiles))
                        msg_j = edge_out[:, k.slot(4), j, 0:D]
                        dve.scalar_tensor_tensor(out=msg_j, in0=typed_bank(j)[:, t * D:(t + 1) * D],
                                                 scalar=grade[:, t, bass.ds(tile, 1)], in1=msg_j,
                                                 op0=ALU.mult, op1=ALU.add).then_inc(s_graded, 1)

                def group_graded(k):
                    if k.outside(EDGE_GROUPS):
                        return
                    dve.wait_ge(s_graded, (GRADES - 1) * NG * (k.n + 1))
                    dve.sem_inc(s_edge_out, 1)

                def rows_out(l, g):
                    if g.outside(NGP):
                        return
                    n = l * NGP + g.n
                    half = slice(NG * g.slot(2), NG * g.slot(2) + NG)
                    m_slot = step_of(g).slot(2)
                    dve.wait_ge(s_back, nth(n))
                    if l < LAYERS - 1:
                        free_rows(l, g)
                        dve.tensor_copy(rows[:, m_slot, half, :],
                                        ps_rows[g.slot(2)][:, :].rearrange("p (j d) -> p j d", j=NG)
                                        ).then_inc(s_rows, 1)
                    else:
                        dve.wait_ge(s_rows, nth(n, 4))
                        dve.wait_ge(s_resid[m_slot], 16 * resid_uses(l, step_of(g)))
                        dve.tensor_tensor(pre[:, g.slot(4), :, :],
                                          ps_rows[g.slot(2)][:, :].rearrange("p (j d) -> p j d", j=NG),
                                          resid[:, m_slot, half, :], ALU.add).then_inc(s_lnsum, 1)

                def statistics(l, g):
                    if g.outside(NGP):
                        return
                    q = (l - LAYERS + 1) * NGP + g.n
                    b = g.slot(4)
                    dve.wait_ge(s_lnsum, nth(q))
                    dve.wait_ge(s_rows, nth(l * NGP + g.n, 4))
                    for j in range(NG):
                        op = dve.bn_stats(ln_stats[:, b, j, :], pre[:, b, j, :])
                    op.then_inc(s_ln, 1)

                def moments(l, g):
                    if g.outside(NGP):
                        return
                    b = g.slot(4)
                    dve.wait_ge(s_ln, (l - LAYERS + 1) * NGP + g.n + 1)
                    dve.sem_inc(s_idle, 1)
                    for j in range(NG):
                        op = dve.bn_aggr(ln_mv[:, b, j, :], ln_stats[:, b, j, :])
                    op.then_inc(s_var, 1)

                def inverse_deviation(l, g):
                    if g.outside(NGP):
                        return
                    dve.wait_ge(s_lnstd, (l - LAYERS + 1) * NGP + g.n + 1)
                    dve.reciprocal(ln_rstd[:, g.slot(4), :], ln_std[:, g.slot(4), :]).then_inc(s_rstd, 1)

                def shift(l, g):
                    if g.outside(NGP):
                        return
                    q = (l - LAYERS + 1) * NGP + g.n
                    b = g.slot(4)
                    dve.wait_ge(s_rstd, q + 1)
                    dve.scalar_tensor_tensor(out=ln_shift[:, b, :], in0=ln_mv[:, b, :, 0], scalar=-1.0,
                                             in1=ln_rstd[:, b, :], op0=ALU.mult, op1=ALU.mult).then_inc(s_shift, 1)

                def degrees(g):
                    if g.outside(NGP):
                        return
                    dve.wait_ge(s_node_p, nth(LAYERS * NGP + g.n))
                    dve.wait_ge(s_next, nth(LAYERS * NGP + g.n, 2))
                    for h, bank in enumerate((ps_node, ps_rows)):
                        op = dve.tensor_scalar(inv_deg[:, g.slot(2), 2 * h:2 * h + 2],
                                               bank[g.slot(2)][:, 0:2 * EW].rearrange("p (j d) -> p j d", j=2)[:, :, D],
                                               1.0, None, ALU.max)
                    op.then_inc(s_degmax, 1)

                def inverse_degrees(g):
                    if g.outside(NGP):
                        return
                    dve.wait_ge(s_degmax, g.n + 1)
                    dve.reciprocal(inv_deg[:, g.slot(2), :], inv_deg[:, g.slot(2), :]).then_inc(s_deg, 1)

                def free_rows(l, g):
                    m = step_of(g)
                    dve.wait_ge(s_store[m.slot(2)], 16 * m.uses(2, STEPS, l))

                for l in range(LAYERS + 1):
                    for k in range(LEAD):
                        if l < LAYERS:
                            first_edges_out(l, At(0, k, BODY))
                            continue
                        for tiles in HALVES:
                            for t in range(1, GRADES):
                                grade_edges(At(0, k, BODY), t, tiles)
                        group_graded(At(0, k, BODY))
                    window_nodes(l, At(0, 0, 2 * BODY))
                    placement(l, At(0, 0, 2 * BODY))

                    def step(m):
                        k = m.plus(LEAD)
                        for b, tiles in enumerate(HALVES):
                            g = first_group(m).plus(b)
                            if l < LAYERS - 1:
                                window_nodes(l, g.plus(1))
                                rows_out(l, g.plus(-2))
                                placement(l, g.plus(1))
                                if not b:
                                    first_edges_out(l, k)
                                continue
                            if l < LAYERS:
                                window_nodes(l, g.plus(1))
                                rows_out(l, g.plus(-2))
                                placement(l, g.plus(1))
                                statistics(l, g.plus(-2))
                                inverse_deviation(l, g.plus(-3))
                                if not b:
                                    first_edges_out(l, k)
                                moments(l, g.plus(-2))
                                shift(l, g.plus(-3))
                                continue
                            of = (k if b else k.plus(-1), HALVES[1 - b])
                            graded_ahead = isinstance(m.n, int) and m.n == 0 and b == 0
                            degrees(g.plus(-1))
                            if not graded_ahead:
                                grade_edges(of[0], 1, of[1])
                            inverse_degrees(g.plus(-1))
                            window_nodes(l, g.plus(1))
                            if not graded_ahead:
                                grade_edges(of[0], 2, of[1])
                            inverse_deviation(l, g.plus(-3))
                            if b == 0 and not graded_ahead:
                                group_graded(of[0])
                            placement(l, g.plus(1))
                            shift(l, g.plus(-3))
                            statistics(l, g.plus(-2))
                            moments(l, g.plus(-2))

                    walk(dve, step)

            dve.wait_ge(s_flag, 1)
            general_needed = dve.value_load(flag[0:1, 0:1], min_val=0, max_val=1)
            with dve.If(general_needed != 0):
                general()
            with dve.Else():
                fast()

        @block.tensor
        def _(pe):
            pe.wait_ge(s_const, 7)
            pe.wait_ge(s_in, 16 * INPUT_LOADS)
            pe.wait_ge(s_meta, 1)
            pe.wait_ge(s_const, 16)
            pe.matmul(ps_rows[0][:, 0:EDGE_TILES], pick_last[:, :], meta[:, :, 1], start=True, stop=True
                      ).then_inc(s_pre, 1)
            pe.wait_ge(s_find, 2)
            pe.matmul(ps_rows[1][0:1, 0:1], bad_sum[:, :], ones_col[:, :], start=True, stop=True
                      ).then_inc(s_pre, 1)

            def general():
                for l, before in edge_loops():
                    with pe.Fori(0, EDGE_TILES) as t:
                        pe.wait_ge(s_gather, 16 * (before + 1 + t))
                        if l == LAYERS:
                            pe.transpose(ps_t[:, 0:D], feats[:, 0:D], ident[:, :]).then_inc(s_ft, 1)
                            pe.wait_ge(s_fte, t + 1)
                            pe.matmul(ps_typed[:, :], feats_t[:, :], typed_w[:, :, :].rearrange("p a b -> p (a b)"),
                                      start=True, stop=True).then_inc(s_typed, 1)
                        pe.wait_ge(s_same, before + 1 + t)
                        pe.wait_ge(s_msg, before + 1 + t)
                        pe.matmul(ps_sum[:, :], same[:, :], (msg if l == LAYERS else feats)[:, :],
                                  start=True, stop=True).then_inc(s_sum, 1)
                    if l == LAYERS:
                        continue
                    loads = NODE_TILES * sum(LOADS[:l])
                    with pe.Fori(0, NODE_TILES) as i:
                        pe.wait_ge(s_load, 16 * loads + 16 * LOADS[l] * (i + 1))
                        pe.transpose(ps_t[:, 0:D], h_in[:, :], ident[:, :])
                        pe.transpose(ps_t[:, D:2 * D], agg_in[:, 0:D], ident[:, :]).then_inc(s_tr, 1)
                        pe.wait_ge(s_tre, l * NODE_TILES + 1 + i)
                        pe.matmul(ps_out[:, :], both_t[:, 0:D], root_w[:, l, :], start=True, stop=False)
                        pe.matmul(ps_out[:, :], both_t[:, D:2 * D], rel_w[:, l, :],
                                  start=False, stop=True).then_inc(s_prod, 1)

            def fast():
                def edge_transposes(l, k):
                    if k.outside(EDGE_GROUPS):
                        return
                    n = l * EDGE_GROUPS + k.n
                    pe.wait_ge(s_gathered[k.slot(4)], 16 * NG * k.uses(4, EDGE_GROUPS, l))
                    pe.wait_ge(s_edge_te, nth(n, 2 if l < LAYERS else 1))
                    for j in range(NG):
                        op = pe.transpose(ps_edge_t[k.slot(2 if l < LAYERS else 1)][:, j * P:(j + 1) * P],
                                          gather_ring[:, k.slot(4), j, :], ident[:, :])
                    op.then_inc(s_edge_t, 1)

                def edge_products(l, k, tiles):
                    if not tiles or k.outside(EDGE_GROUPS):
                        return
                    n = l * EDGE_GROUPS + k.n
                    pe.wait_ge(s_edge_te, nth(n))
                    if l < LAYERS:
                        pe.wait_ge(s_edge_out, nth(n, 2))
                        for j in tiles:
                            op = pe.matmul(ps_edge_out[k.slot(2)][:, j * D:(j + 1) * D],
                                           edge_t[:, k.slot(2), j * P:(j + 1) * P], rel_w[:, l, :],
                                           start=True, stop=True)
                        op.then_inc(s_edge_p, 1)
                        return
                    for j in tiles:
                        tile = NG * k.n + j
                        last = graded_last(k, j)
                        if not (isinstance(last, int) and last <= 0):
                            pe.wait_ge(s_graded, last)
                        bank = typed_bank(j)[:, 0:GRADES * D]
                        pe.matmul(bank, edge_t[:, k.slot(2), j * P:(j + 1) * P],
                                  typed_w[:, :, :].rearrange("p a b -> p (a b)"), start=True, stop=False)
                        pe.matmul(bank, bias_ones[0:BIAS_PARTS, :], bias_parts[0:BIAS_PARTS, :],
                                  start=False, stop=True).then_inc(s_typed_p, 1)

                def nodes(l, g):
                    if g.outside(NGP):
                        return
                    n = l * NGP + g.n
                    bank = ps_node[g.slot(2)]
                    pe.wait_ge(s_next, nth(n, 2))
                    if l < LAYERS:
                        if l == 0 or not g.kept:
                            pe.wait_ge(s_feat[g.slot(4) // 2], 16 * feat_uses(l, step_of(g)))
                            feats_g = feat_t[:, g.slot(4) // 2, GD * (g.c % 2):GD * (g.c % 2 + 1)]
                        else:
                            feats_g = kept[:, bass.ds(GD * g.n, GD)]
                        pe.matmul(bank[:, :], root_w[:, l, :], feats_g, start=True, stop=False)
                    pe.wait_ge(s_place, nth(n))
                    kind = wins(l)
                    for j, (lo, hi) in enumerate(kind.spans):
                        rows_j = win[0:kind.edges, g.slot(4), j, :]
                        place_j = place[0:kind.edges, g.slot(4), lo:hi]
                        if l < LAYERS:
                            op = pe.matmul(bank[:, lo:hi], rows_j[:, 0:D], place_j, start=False,
                                           stop=(j == kind.count - 1))
                        else:
                            typed_bank = (ps_node, ps_rows)[j // 2][g.slot(2)]
                            op = pe.matmul(typed_bank[:, (j % 2) * EW:(j % 2 + 1) * EW], place_j, rows_j,
                                           start=True, stop=True)
                    op.then_inc(s_node_p, 1)

                def transposes_back(l, g):
                    if l == LAYERS or g.outside(NGP):
                        return
                    n = l * NGP + g.n
                    pe.wait_ge(s_next, nth(n))
                    if l < LAYERS - 1:
                        pe.wait_ge(s_rows, nth(n, 2))
                    elif not (isinstance(g.n, int) and g.n < 2):
                        pe.wait_ge(s_lnsum, nth(g.n, 2))
                    for j in range(NG):
                        op = pe.transpose(ps_rows[g.slot(2)][:, j * D:(j + 1) * D],
                                          next_t[:, g.slot(4), j * P:(j + 1) * P], ident[:, :])
                    op.then_inc(s_back, 1)

                for l in range(LAYERS + 1):
                    if l:
                        pe.wait_ge(s_next, nth(l * NGP - 1))
                        if l < LAYERS:
                            pe.wait_ge(s_rows, nth(l * NGP - 1))
                        else:
                            pe.wait_ge(s_lnsum, nth(NGP - 1))
                            pe.wait_ge(s_bias, 1)
                        pe.wait_ge(s_edge_out, nth(l * EDGE_GROUPS - 1))
                    edge_transposes(l, At(0, 0, BODY))
                    for k in range(LEAD):
                        edge_transposes(l, At(0, k + 1, BODY))
                        for tiles in first_halves(l):
                            edge_products(l, At(0, k, BODY), tiles)

                    def step(m):
                        for b, tiles in enumerate(first_halves(l)):
                            g = first_group(m).plus(b)
                            if l == LAYERS:
                                nodes(l, g)
                            if b:
                                edge_transposes(l, m.plus(LEAD + 1))
                            edge_products(l, m.plus(LEAD), tiles)
                            if l < LAYERS:
                                nodes(l, g)
                            transposes_back(l, g.plus(-1))

                    walk(pe, step)

            pe.wait_ge(s_flag, 1)
            general_needed = pe.value_load(flag[0:1, 0:1], min_val=0, max_val=1)
            with pe.If(general_needed != 0):
                general()
            with pe.Else():
                fast()

        @block.scalar
        def _(act):
            def general():
                for l, before in edge_loops():
                    with act.Fori(0, EDGE_TILES) as t:
                        if l == LAYERS:
                            act.wait_ge(s_ft, t + 1)
                            act.activation(feats_t[:, :], ps_t[:, 0:D], ACT.Copy).then_inc(s_fte, 1)
                        act.wait_ge(s_sum, before + 1 + t)
                        act.activation(summed[:, :], ps_sum[:, :], ACT.Copy).then_inc(s_summed, 1)
                    with act.Fori(0, NODE_TILES) as i:
                        if l < LAYERS:
                            act.wait_ge(s_tr, l * NODE_TILES + 1 + i)
                            act.activation(both_t[:, :], ps_t[:, :], ACT.Copy).then_inc(s_tre, 1)
                        if l >= LAYERS - 1:
                            act.wait_ge(s_z, (l - LAYERS + 1) * NODE_TILES + 1 + i)
                            act.activation(std[:, :], mean_var[:, 1:2], ACT.Sqrt,
                                           bias=eps_col[:, 0:1]).then_inc(s_std, 1)

            def fast():
                act.wait_ge(s_in, 16 * INPUT_LOADS)
                act.wait_ge(s_const, 16)

                def edge_copy(l, k):
                    if k.outside(EDGE_GROUPS):
                        return
                    n = l * EDGE_GROUPS + k.n
                    act.wait_ge(s_edge_t, n + 1)
                    act.wait_ge(s_edge_out, nth(n, 2))
                    act.activation(edge_t[:, k.slot(2), :], ps_edge_t[k.slot(2 if l < LAYERS else 1)][:, :], ACT.Copy
                                   ).then_inc(s_edge_te, 1)

                def first_grade(l, k, tiles):
                    if l < LAYERS or k.outside(EDGE_GROUPS):
                        return
                    for j in tiles:
                        tile = NG * k.n + j
                        act.wait_ge(s_typed_p, tile + 1)
                        act.wait_ge(s_edge_st[k.slot(4)], 16 * k.uses(4, EDGE_GROUPS, l))
                        act.activation(edge_out[:, k.slot(4), j, 0:D], typed_bank(j)[:, 0:D], ACT.Copy,
                                       scale=grade[:, 0, bass.ds(tile, 1)]).then_inc(s_first, 1)

                def write_edges(l, k):
                    if k.outside(EDGE_GROUPS):
                        return
                    n = l * EDGE_GROUPS + k.n
                    act.wait_ge(s_edge_out, nth(n))
                    act.wait_ge(s_edge_meta, nth(n))
                    act.dma_start(edge_groups[bass.ds(k.n, 1)].squeeze(0), edge_out[:, k.slot(4), :, :]
                                  ).then_inc(s_edge_st[k.slot(4)], 16)

                def features(l, g):
                    if g.outside(NGP):
                        return
                    n = l * NGP + g.n
                    b = g.slot(2)
                    act.wait_ge(s_node_p, nth(n))
                    if l == LAYERS:
                        act.wait_ge(s_deg, nth(g.n))
                        act.wait_ge(s_lnsum, nth(NGP + g.n, 4))
                        for j in range(NG):
                            bank = (ps_node, ps_rows)[j // 2][b]
                            op = act.activation(next_t[:, g.slot(4), j * D:(j + 1) * D],
                                                bank[:, (j % 2) * EW:(j % 2) * EW + D],
                                                ACT.Relu, scale=inv_deg[:, b, j:j + 1])
                        op.then_inc(s_next, 1)
                        return
                    func = ACT.Relu if l < LAYERS - 1 else ACT.Identity
                    if l < LAYERS - 1 and g.kept:
                        act.activation(kept[:, bass.ds(GD * g.n, GD)], ps_node[b][:, :], func,
                                       bias=rel_bt[:, l:l + 1])
                    act.wait_ge(s_back, nth(n, 4))
                    m = step_of(g)
                    act.wait_ge(s_spill[m.slot(2)], 16 * spills_before(l, m))
                    act.activation(next_t[:, g.slot(4), :], ps_node[b][:, :], func,
                                   bias=rel_bt[:, l:l + 1]).then_inc(s_next, 1)

                def spill_step(l, m):
                    if l >= LAYERS - 1 or m.outside(STEPS) or m.kept:
                        return
                    act.wait_ge(s_next, nth(l * NGP + 2 * m.n + 1))
                    act.dma_start(spill[bass.ds(m.n, 1)].squeeze(0),
                                  next_t[:, 2 * m.slot(2):2 * m.slot(2) + 2, :].rearrange("p g n -> p (g n)")
                                  ).then_inc(s_spill[m.slot(2)], 16)

                def load_features(l, m):
                    if m.outside(STEPS) or l == LAYERS or (l > 0 and m.kept):
                        return
                    of = spill if l else x_t
                    act.dma_start(feat_t[:, m.slot(2), :], of[bass.ds(m.n, 1)].squeeze(0)
                                 ).then_inc(s_feat[m.slot(2)], 16)

                def load_residual(l, m):
                    if m.outside(STEPS) or l < LAYERS - 1 or (l == LAYERS and m.kept):
                        return
                    used = nth((l - LAYERS + 1) * NGP + 2 * m.n, 3)
                    if not (isinstance(m.n, int) and m.n < 2):
                        act.wait_ge(s_lnsum, used)
                    of = h_steps[0] if l < LAYERS else h_steps[LAYERS]
                    act.dma_start(resid[:, m.slot(2), :, :], of[bass.ds(m.n, 1)].squeeze(0)
                                 ).then_inc(s_resid[m.slot(2)], 16)

                def deviation(l, g):
                    if l < LAYERS - 1 or g.outside(NGP):
                        return
                    q = (l - LAYERS + 1) * NGP + g.n
                    act.wait_ge(s_var, q + 1)
                    act.activation(ln_std[:, g.slot(4), :], ln_mv[:, g.slot(4), :, 1], ACT.Sqrt,
                                   bias=eps_col[:, 0:1]).then_inc(s_lnstd, 1)

                def normalise(l, g):
                    if l < LAYERS - 1 or g.outside(NGP):
                        return
                    q = (l - LAYERS + 1) * NGP + g.n
                    b = g.slot(4)
                    m = step_of(g)
                    act.wait_ge(s_shift, q + 1)
                    act.wait_ge(s_store[m.slot(2)], 16 * m.uses(2, STEPS, l))
                    for j in range(NG):
                        if l == LAYERS - 1 and g.kept:
                            to = kept[:, bass.ds(GD * g.n + j * D, D)]
                        else:
                            to = rows[:, m.slot(2), NG * g.slot(2) + j, :]
                        op = act.activation(to, pre[:, b, j, :], ACT.Identity, bias=ln_shift[:, b, j:j + 1],
                                            scale=ln_rstd[:, b, j:j + 1])
                    op.then_inc(s_rows, 1)

                def store(l, m):
                    if m.outside(STEPS):
                        return
                    act.wait_ge(s_rows, nth(l * NGP + 2 * m.n + 1))
                    if l == LAYERS - 1 and m.kept:
                        of = kept[:, bass.ds(2 * GD * m.n, 2 * GD)].rearrange("p (j d) -> p j d", j=2 * NG)
                    else:
                        of = rows[:, m.slot(2), :, :]
                    act.dma_start(h_steps[l + 1][bass.ds(m.n, 1)].squeeze(0), of).then_inc(s_store[m.slot(2)], 16)

                for l in range(LAYERS + 1):
                    if l:
                        for b in range(4):
                            act.wait_ge(s_win[b], 16 * THIRDS.count * l * count(b, 4, NGP))
                        for b in range(2):
                            act.wait_ge(s_spill[b], 16 * (1 + spills(l, b)))
                    load_features(l, At(0, 0, BODY))
                    edge_copy(l, At(0, 0, BODY))
                    for k in range(LEAD):
                        edge_copy(l, At(0, k + 1, BODY))
                        first_grade(l, At(0, k, BODY), range(NG))
                        write_edges(l, At(0, k, BODY))

                    def step(m):
                        for b, tiles in enumerate(first_halves(l)):
                            g = first_group(m).plus(b)
                            deviation(l, g.plus(-3))
                            features(l, g.plus(-1))
                            if not b and l < LAYERS - 1:
                                store(l, m.plus(-2))
                            if not b:
                                if l and isinstance(m.n, int) and m.n == RES_STEPS:
                                    load_features(l, m)
                                load_features(l, m.plus(1))
                                load_residual(l, m)
                            if b:
                                if l < LAYERS:
                                    write_edges(l, m.plus(LEAD))
                                edge_copy(l, m.plus(LEAD + 1))
                            normalise(l, g.plus(-4))
                            first_grade(l, m.plus(LEAD), tiles)
                            if b and l >= LAYERS - 1:
                                store(l, m.plus(-2))
                            if not b:
                                spill_step(l, m.plus(-1))
                                if l == LAYERS and not (isinstance(m.n, int) and m.n < 1):
                                    write_edges(l, m.plus(LEAD - 1))

                    walk(act, step)

            act.wait_ge(s_flag, 1)
            general_needed = act.value_load(flag[0:1, 0:1], min_val=0, max_val=1)
            with act.If(general_needed != 0):
                general()
            with act.Else():
                fast()


def kernel(**inputs):
    import numpy as _np
    import concourse.bacc as _bacc
    from concourse import mybir as _mybir
    from concourse.bass_utils import run_bass_kernel_spmd as _run

    a = {k: _np.asarray(v) for k, v in inputs.items()}

    def padded(v, rows, fill=0):
        tail = _np.full((rows - v.shape[0],) + v.shape[1:], fill, v.dtype)
        return _np.concatenate([v, tail])

    def by_tile(v, fill=0):
        return _np.ascontiguousarray(padded(v, SLOTS, fill).reshape(EDGE_TILES, P).T)

    arrays = {
        "in_x": padded(a["x"], ROWS),
        "in_x_t": _np.ascontiguousarray(padded(a["x"], ROWS).reshape(STEPS, 2 * GD, D).transpose(0, 2, 1)),
        "in_src": by_tile(a["src"]),
        "in_dst": by_tile(a["dst"], PAD_DST),
        "in_dst_rows": padded(a["dst"], SLOTS + P, PAD_DST).reshape(EDGE_TILES + 1, P),
        "in_type": by_tile(a["edge_type_30"]),
        "in_weight": by_tile(a["edge_weight"]),
        "in_w_rel": a["L0_gnn_W_rel"], "in_b_rel": a["L0_gnn_b_rel"], "in_w_root": a["L0_gnn_W_root"],
        "in_w_typed": a["L1_gnn_W"], "in_b_typed": a["L1_gnn_b"],
    }
    nc = _bacc.Bacc("TRN2", target_bir_lowering=False, num_devices=1)
    args = [nc.dram_tensor(n, v.shape, _mybir.dt.from_np(v.dtype), kind="ExternalInput").ap()
            for n, v in arrays.items()]
    args.append(nc.dram_tensor("out_x", (ROWS, D), _mybir.dt.float32, kind="ExternalOutput").ap())
    gnn_kernel(nc, *args)
    r = _run(nc, [arrays], core_ids=[0])
    return r.results[0]["out_x"][:NODES]
```
